# Optimizing a Trainium2 kernel written in Bass

```python
import numpy as np
import jax
import jax.numpy as jnp

def _softmax(x, axis=-1):
    return jax.nn.softmax(x, axis=axis)

def _gelu(x):
    return jax.nn.gelu(x, approximate=True)

def _silu(x):
    return jax.nn.silu(x)

def _sigmoid(x):
    return jax.nn.sigmoid(x)

def _layernorm(x, axis=-1, eps=1e-05):
    m = jnp.mean(x, axis=axis, keepdims=True)
    v = jnp.var(x, axis=axis, keepdims=True)
    return (x - m) / jnp.sqrt(v + eps)

def _scatter_add(tgt, idx, src, axis=0):
    return tgt.at[idx].add(src)

def _segment_sum(src, seg, n):
    return jax.ops.segment_sum(src, seg, n)
kernel_name = 'mk_seq_postln_d1_jaxref_r8_33ce8c'

def setup_inputs(seed: int=0):
    np.random.seed(seed)
    _w = jnp.asarray

    def _L0_attn_setup():
        import math
        import jax, jax.numpy as jnp
        import numpy as np
        B, C, D = (4, 256, 128)
        DQ = DV = 64
        H = 16
        key = jax.random.key(seed)
        kx, kq, kk, kv, kw = jax.random.split(key, 5)
        x = jax.random.normal(kx, (B, C, D), dtype=jnp.float32)
        Q = jax.random.normal(kq, (DQ, D, H), dtype=jnp.float32) / math.sqrt(D)
        K = jax.random.normal(kk, (DQ, D, H), dtype=jnp.float32) / math.sqrt(D)
        V = jax.random.normal(kv, (DV, D, H), dtype=jnp.float32) / math.sqrt(D)
        W = jax.random.normal(kw, (D, DV, H), dtype=jnp.float32) / math.sqrt(DV)
        return {'x': x, 'Q': Q, 'K': K, 'V': V, 'W': W}
    _L0_attn_in = _L0_attn_setup()

    def _L0_ffn_setup():
        import jax, jax.numpy as jnp
        import numpy as np
        TOP_K = 2
        key = jax.random.key(seed)
        k1, k2, k3, k4 = jax.random.split(key, 4)
        B, T, D, F, E = (2, 128, 128, 256, 8)
        x = jax.random.normal(k1, (B, T, D), dtype=jnp.float32)
        Wg = jax.random.normal(k2, (D, E), dtype=jnp.float32) * 0.02
        W1 = jax.random.normal(k3, (E, D, F), dtype=jnp.float32) * 0.02
        W2 = jax.random.normal(k4, (E, F, D), dtype=jnp.float32) * 0.02
        return {'x': x, 'Wg': Wg, 'W1': W1, 'W2': W2}
    _L0_ffn_in = _L0_ffn_setup()
    _d = {'L0_attn_x': _L0_attn_in['x'], 'L0_attn_Q': _L0_attn_in['Q'], 'L0_attn_K': _L0_attn_in['K'], 'L0_attn_V': _L0_attn_in['V'], 'L0_attn_W': _L0_attn_in['W'], 'L0_ffn_Wg': _L0_ffn_in['Wg'], 'L0_ffn_W1': _L0_ffn_in['W1'], 'L0_ffn_W2': _L0_ffn_in['W2']}
    _x0 = _d['L0_attn_x']
    _d['L0_attn_x'] = jax.random.normal(jax.random.fold_in(jax.random.key(seed), 1), (4, 512, 128), dtype=_x0.dtype)
    del _x0
    return _d

def reference(L0_attn_x, L0_attn_Q, L0_attn_K, L0_attn_V, L0_attn_W, L0_ffn_Wg, L0_ffn_W1, L0_ffn_W2):

    def _L0_attn_ref(x, Q, K, V, W):
        import math
        import jax, jax.numpy as jnp
        import numpy as np
        B, C, D = (4, 256, 128)
        DQ = DV = 64
        H = 16
        d_query, d_embed, num_heads = Q.shape
        d_value = V.shape[0]
        sq = math.sqrt(d_query / d_embed)
        sv = math.sqrt(d_value / d_embed)
        q = jnp.einsum('qdh,bcd->bhcq', Q, x) * sq
        k = jnp.einsum('qdh,bcd->bhcq', K, x) * sq
        v = jnp.einsum('vdh,bcd->bhcv', V, x) * sv
        att = jnp.einsum('bhcq,bhCq->bhcC', q, k) / d_query
        T = x.shape[1]
        causal = jnp.arange(T)[:, None] >= jnp.arange(T)[None, :]
        att = jnp.where(causal, att, -jnp.inf)
        p = jax.nn.softmax(att, axis=-1)
        y = jnp.einsum('bhcC,bhCv->bhcv', p, v)
        z = jnp.einsum('dvh,bhcv->bcd', W, y) * (math.sqrt(d_embed / d_value) / num_heads)
        return z

    def _L0_ffn_ref(x, Wg, W1, W2):
        import jax, jax.numpy as jnp
        import numpy as np
        TOP_K = 2
        B, T, D = x.shape
        E = Wg.shape[-1]
        xt = x.reshape(B * T, D)
        logits = xt @ Wg
        probs = jax.nn.softmax(logits, axis=-1)
        topw, topi = jax.lax.top_k(probs, TOP_K)
        topw = topw / jnp.sum(topw, axis=-1, keepdims=True)
        combine = jnp.sum(jax.nn.one_hot(topi, E, dtype=xt.dtype) * topw[..., None], axis=1)
        h = jax.nn.relu(jnp.einsum('nd,edf->enf', xt, W1))
        y = jnp.einsum('enf,efd->end', h, W2)
        out = jnp.einsum('ne,end->nd', combine, y)
        return out.reshape(B, T, D)
    x = L0_attn_x
    x = _layernorm(x + _L0_attn_ref(x, L0_attn_Q, L0_attn_K, L0_attn_V, L0_attn_W), axis=-1)
    x = _layernorm(x + _L0_ffn_ref(x, L0_ffn_Wg, L0_ffn_W1, L0_ffn_W2), axis=-1)
    return x

_drawn_inputs = setup_inputs


def setup_inputs(seed=0):
    import zlib

    import numpy as np

    out = dict(_drawn_inputs(seed))
    spreads = {}
    factors = {'L0_attn_Q': 8.0, 'L0_attn_K': 8.0}
    for name, (base, spread) in spreads.items():
        noise = np.random.default_rng([zlib.crc32(name.encode()), seed]).standard_normal(out[name].shape)
        drawn = base * np.exp(spread * noise) if base else spread * noise
        out[name] = jnp.asarray(drawn.astype(out[name].dtype))
    for name, factor in factors.items():
        out[name] = (out[name] * factor).astype(out[name].dtype)
    return out
```

```python
from contextlib import ExitStack

import concourse.bass as bass
from concourse import mybir

F32 = mybir.dt.float32
F32R = mybir.dt.float32r
F16 = mybir.dt.float16
BF16 = mybir.dt.bfloat16
U32 = mybir.dt.uint32
ALU = mybir.AluOpType
ACT = mybir.ActivationFunctionType
X = mybir.AxisListType.X

P = 128
BANK = 512
EPS = 1e-5
MASKED = -1e30


def post_ln_layer(nc, x, Q, K, V, W, Wg, W1, W2, out):
    B, T, D = x.shape
    DQ, _, H = Q.shape
    DV = V.shape[0]
    E, _, F = W1.shape
    QT = T // P
    HP = H // 2
    FT = E * F // P
    FPE = F // P
    TOP = 2
    NBLK = QT * (QT + 1) // 2
    VW = DV + 2
    QK_SCALE = (DQ / D) / DQ
    Z_SCALE = 1.0 / H
    assert D == P and T == BANK and DQ == DV == 64 and E == 8

    def blk(i, j):
        return i * (i + 1) // 2 + j

    S_AT = [(2, 0), (2, 256), (1, 0), (0, 0)]
    S_COLS = [256, 256, 384, 512]
    PT_PIECES = [(0, 4), (4, NBLK)]

    a_dram = nc.dram_tensor("a_parts", (H, P, 2 * P), F32).ap()
    xt_dram = nc.dram_tensor("xt_parts", (B, P, 2, T), F32).ap()

    x_tiles = x.rearrange("b (t p) d -> b p t d", p=P)
    out_tiles = out.rearrange("b (t p) d -> b p t d", p=P)

    with ExitStack() as ctx:
        def sb(name, shape, dt, c=ctx):
            return c.enter_context(nc.sbuf_tensor(name, shape, dt))

        def sem(name):
            return ctx.enter_context(nc.semaphore(name))

        ps_s = ctx.enter_context(nc.psum_tensor("ps_s", [P, 3, BANK], F32))
        ps_t = ctx.enter_context(nc.psum_tensor("ps_t", [P, 3, BANK], F32))
        ps_g = ctx.enter_context(nc.psum_tensor("ps_g", [P, BANK], F32))
        ps_y = ctx.enter_context(nc.psum_tensor("ps_y", [P, BANK], F32))

        ident = sb("ident", [P, P], F32)
        mask = sb("mask", [P, T], F32)
        iota8 = sb("iota8", [P, QT, E], F32)
        eps_in = sb("eps_in", [P, 2, QT], F32)
        wg = sb("wg", [P, E], F32)
        vt = sb("vt", [P, 2, H * DV], F32R)
        wc = sb("wc", [P, 2, HP * D], F32R)
        w1 = sb("w1", [P, 2, E * F], F32R)
        w2 = sb("w2", [P, 2, FT * D], F32R)
        sel = sb("sel", [E, E * P], F32R)

        s_in = [sem(f"loaded_{n}") for n in ("x", "q", "k", "v", "w", "w1", "w2", "wg")]
        in_x, in_q, in_k, in_v, in_w, in_w1, in_w2, in_wg = s_in
        const_step = sem("const_step")
        setup_filled = sem("setup_filled")
        setup_hi = sem("setup_hi")
        setup_lo = sem("setup_lo")
        w_hi = sem("w_hi")
        w_lo = sem("w_lo")
        w_sorted = sem("w_sorted")
        scratch_out = sem("scratch_out")

        with ExitStack() as sctx:
            x_raw = sb("x_raw", [P, B * QT, D], F32, sctx)
            q_raw = sb("q_raw", [DQ, D * H], F32, sctx)
            k_raw = sb("k_raw", [DQ, D * H], F32, sctx)
            v_raw = sb("v_raw", [DV, D * H], F32, sctx)
            w_raw = sb("w_raw", [D, DV * H], F32, sctx)
            w1_raw = sb("w1_raw", [P, E * F], F32, sctx)
            w2_raw = sb("w2_raw", [P, FT * D], F32, sctx)
            sel_raw = sb("sel_raw", [E, E * P], F32, sctx)
            a_all = sb("a_all", [P, H, 2, P], F32R, sctx)
            xt_all = sb("xt_all", [P, B, 2, T], F32R, sctx)

            q_h = q_raw[:, :].rearrange("q (d h) -> q h d", h=H)
            k_h = k_raw[:, :].rearrange("q (d h) -> q h d", h=H)
            v_h = v_raw[:, :].rearrange("v (d h) -> v h d", h=H)
            w_h = sb("w_h", [D, H * DV], F32, sctx)

            def setup_bank(k):
                k = k % 8
                return ps_s[:, k, :] if k < 3 else ps_t[:, k - 3, :] if k < 6 else ps_g[:, :] if k == 6 else ps_y[:, :]

            jobs = [("x", b) for b in range(B)] + [("a", q) for q in range(H // 4)] + \
                   [("v", i) for i in range(2)] + [("w", i) for i in range(2)]

            def job_out(kind, n, part):
                if kind == "x":
                    return xt_all[:, n, part, :], 1.0
                if kind == "a":
                    return a_all[:, 4 * n:4 * n + 4, part, :], QK_SCALE
                if kind == "v":
                    return vt[:, part, n * BANK:(n + 1) * BANK], 1.0
                return wc[:, part, n * BANK:(n + 1) * BANK], Z_SCALE

            def job_in(k, kind):
                bank = setup_bank(k)
                return bank.rearrange("p (h d) -> p h d", h=4) if kind == "a" else bank

            with nc.Block() as block:
                @block.sync
                def _(sp):
                    sp.dma_start(x_raw[:, :, :], x.rearrange("b (t p) d -> p (b t) d", p=P)).then_inc(in_x, 16)
                    sp.dma_start(v_raw[:, :], V.rearrange("v d h -> v (d h)")).then_inc(in_v, 16)
                    sp.dma_start(w1_raw[:, :].rearrange("d (e f) -> d e f", e=E),
                                 W1.rearrange("e d f -> d e f")).then_inc(in_w1, 16)
                    sp.wait_ge(setup_hi, B)
                    sp.wait_ge(setup_lo, B)
                    sp.dma_start(xt_dram.rearrange("b p k t -> p b k t"), xt_all[:, :, :, :].bitcast(F32)).then_inc(scratch_out, 16)
                    sp.wait_ge(setup_hi, B + H // 4)
                    sp.wait_ge(setup_lo, B + H // 4)
                    sp.dma_start(a_dram.rearrange("h p c -> p h c"),
                                 a_all[:, :, :, :].bitcast(F32).rearrange("p h k c -> p h (k c)")).then_inc(scratch_out, 16)
                    sp.wait_ge(scratch_out, 32)

                @block.gpsimd
                def _(pool):
                    pool.memset(ident[:, :], 0.0).then_inc(const_step, 1)
                    pool.wait_ge(const_step, 1)
                    pool.affine_select(out=ident[:, :], in_=ident[:, :], compare_op=ALU.not_equal, fill=1.0, base=0,
                                       pattern=[[-1, P]], channel_multiplier=1).then_inc(const_step, 1)
                    pool.memset(mask[:, :], 0.0).then_inc(const_step, 1)
                    pool.memset(sel_raw[:, :], 1.0).then_inc(const_step, 1)
                    pool.memset(eps_in[:, 1, :], -0.5).then_inc(const_step, 1)
                    pool.iota(iota8[:, :, :], pattern=[[0, QT], [1, E]], base=0, channel_multiplier=0,
                              allow_small_or_imprecise_dtypes=True).then_inc(const_step, 1)
                    pool.wait_ge(const_step, 3)
                    pool.affine_select(out=mask[:, T - P:T], in_=mask[:, T - P:T], compare_op=ALU.is_ge, fill=MASKED,
                                       base=0, pattern=[[-1, P]], channel_multiplier=1).then_inc(const_step, 1)
                    pool.wait_ge(const_step, 4)
                    pool.affine_select(out=sel_raw[:, :].rearrange("p (e c) -> p e c", e=E),
                                       in_=sel_raw[:, :].rearrange("p (e c) -> p e c", e=E),
                                       compare_op=ALU.is_equal, fill=0.0, base=0, pattern=[[-1, E], [0, P]],
                                       channel_multiplier=1).then_inc(const_step, 1)
                    pool.wait_ge(w_hi, 1)
                    pool.tensor_tensor(w1[:, 1, :], w1_raw[:, :], w1[:, 0, :], ALU.subtract).then_inc(w_lo, 1)
                    pool.wait_ge(w_hi, 2)
                    pool.tensor_tensor(w2[:, 1, :], w2_raw[:, :], w2[:, 0, :], ALU.subtract).then_inc(w_lo, 1)
                    pool.wait_ge(w_lo, 2)

                @block.scalar
                def _(act):
                    act.dma_start(q_raw[:, :], Q.rearrange("q d h -> q (d h)")).then_inc(in_q, 16)
                    act.dma_start(k_raw[:, :], K.rearrange("q d h -> q (d h)")).then_inc(in_k, 16)
                    act.dma_start(w_raw[:, :], W.rearrange("d v h -> d (v h)")).then_inc(in_w, 16)
                    act.dma_start(w2_raw[:, :].rearrange("f (c d) -> f c d", d=D),
                                  W2.rearrange("e (c f) d -> f (e c) d", f=P)).then_inc(in_w2, 16)
                    act.dma_start(wg[:, :], Wg).then_inc(in_wg, 16)
                    for k, (kind, n) in enumerate(jobs):
                        act.wait_ge(setup_filled, k + 1)
                        dst, scale = job_out(kind, n, 0)
                        nc.scalar.activation(dst, job_in(k, kind), ACT.Copy, scale=scale).then_inc(setup_hi, 1)
                    act.wait_ge(in_w1, 16)
                    nc.scalar.activation(w1[:, 0, :], w1_raw[:, :], ACT.Copy).then_inc(w_hi, 1)
                    act.wait_ge(in_w2, 16)
                    nc.scalar.activation(w2[:, 0, :], w2_raw[:, :], ACT.Copy).then_inc(w_hi, 1)
                    act.wait_ge(const_step, 8)
                    nc.scalar.activation(sel[:, :], sel_raw[:, :], ACT.Copy).then_inc(w_hi, 1)
                    act.wait_ge(w_hi, 3)
                    act.wait_ge(in_wg, 16)

                @block.vector
                def _(dve):
                    for k, (kind, n) in enumerate(jobs):
                        if (kind, n) == ("v", 0):
                            dve.wait_ge(in_w, 16)
                            nc.vector.tensor_copy(w_h[:, :].rearrange("d (h v) -> d h v", h=H),
                                                  w_raw[:, :].rearrange("d (v h) -> d h v", h=H)).then_inc(w_sorted, 1)
                        dve.wait_ge(setup_hi, k + 1)
                        dst, scale = job_out(kind, n, 1)
                        nc.vector.scalar_tensor_tensor(out=dst, in0=job_in(k, kind), scalar=scale,
                                                       in1=job_out(kind, n, 0)[0], op0=ALU.mult,
                                                       op1=ALU.subtract).then_inc(setup_lo, 1)
                    dve.wait_ge(setup_lo, len(jobs))

                @block.tensor
                def _(pe):
                    pe.wait_ge(const_step, 2)
                    loaded = {"x": [in_x], "a": [in_q, in_k], "v": [in_v], "w": []}
                    for k, (kind, n) in enumerate(jobs):
                        if n == 0:
                            for s in loaded[kind]:
                                pe.wait_ge(s, 16)
                        if kind == "w":
                            pe.wait_ge(w_sorted, 1)
                        if k >= 8:
                            pe.wait_ge(setup_lo, k - 7)
                        bank = setup_bank(k)
                        if kind == "x":
                            for t in range(QT):
                                last = nc.tensor.transpose(bank[:, t * P:(t + 1) * P], x_raw[:, n * QT + t, :],
                                                           ident[:, :])
                        elif kind == "a":
                            for h in range(4):
                                last = nc.tensor.matmul(bank[:, h * P:(h + 1) * P], q_h[:, 4 * n + h, :],
                                                        k_h[:, 4 * n + h, :], start=True, stop=True)
                        elif kind == "v":
                            for h in range(8):
                                last = nc.tensor.transpose(bank[:, h * DV:(h + 1) * DV], v_h[:, 8 * n + h, :],
                                                           ident[0:DV, 0:DV])
                        else:
                            for c in range(4):
                                last = nc.tensor.transpose(bank[:, c * P:(c + 1) * P], w_h[:, (4 * n + c) * P:(4 * n + c + 1) * P],
                                                           ident[:, :])
                        last.then_inc(setup_filled, 1)

        a_st = sb("a_st", [P, 2, 2 * P], F32R)
        xt = sb("xt", [P, 2, 2, T], F32R)
        xv = sb("xv", [P, 2, P], F32R)
        x_nat = sb("x_nat", [P, QT, D], F32)
        v1 = sb("v1", [P, 2, QT, H, VW], BF16)
        v2 = sb("v2", [P, 2, QT, H, DV], BF16)
        v3 = sb("v3", [P, 2, QT, H, DV], BF16)
        v_full = sb("v_full", [P, BANK], F32)
        v_rest = sb("v_rest", [P, BANK], F32)
        zeros = sb("zeros", [P, BANK], F32)
        g_hi = sb("g_hi", [P, 2, T], F32R)
        g_lo = sb("g_lo", [P, 2, T], F32R)
        neg_s = sb("neg_s", [P, 2, NBLK * P], F32)
        neg_max = sb("neg_max", [P, 2, QT], F32)
        p = sb("p", [P, 2, NBLK * P], F32)
        pt_hi = sb("pt_hi", [P, 2, NBLK * P], F16)
        pt_lo = sb("pt_lo", [P, 2, NBLK * P], F16)
        y = sb("y", [P, QT, H * DV], F32)
        r_sum = sb("r_sum", [P, 2, QT], F32)
        act_hi = sb("act_hi", [P, 3, BANK], F32R)
        act_lo = sb("act_lo", [P, 3, BANK], F32R)
        col = sb("col", [P, BANK], F32)
        res = sb("res", [P, QT, D], F32)
        x1 = sb("x1", [P, QT, D], F32)
        x1t = sb("x1t", [P, T], F32)
        x1t_hi = sb("x1t_hi", [P, T], F32R)
        x1t_lo = sb("x1t_lo", [P, T], F32R)
        x2 = sb("x2", [P, QT, D], F32)
        st = sb("st", [P, QT, 6], F32)
        mv = sb("mv", [P, QT, 2], F32)
        rstd = sb("rstd", [P, QT], F32)
        logit = sb("logit", [P, QT, E], F32)
        best = sb("best", [P, QT, E], F32)
        best_at = sb("best_at", [P, QT, E], U32)
        at_f = sb("at_f", [P, QT, TOP], F32)
        gate = sb("gate", [P, 5, QT], F32)
        pick = sb("pick", [P, 2, QT, E], F32)
        comb = sb("comb", [P, QT, E], F32)
        ct_hi = sb("ct_hi", [E, T], F32R)
        ct_lo = sb("ct_lo", [E, T], F32R)
        p_flat = p[:, :, :].rearrange("p k c -> p (k c)")
        hid = [p_flat[:, i * BANK:(i + 1) * BANK] for i in range(3)]
        c_row = [p_flat[:, (3 + i) * BANK:(4 + i) * BANK] for i in range(2)]

        a_in = [sem(f"a_in_{k}") for k in range(2)]
        xt_in = sem("xt_in")
        xv_in = sem("xv_in")
        x_in = sem("x_in")
        out_stored = sem("out_stored")
        const2 = sem("const2")
        wait_carrier = sem("wait_carrier")
        g_filled, g_hi_done, g_lo_done = sem("g_filled"), sem("g_hi_done"), sem("g_lo_done")
        s_filled, max_done, exp_done = sem("s_filled"), sem("max_done"), sem("exp_done")
        pt_filled, pt_hi_done, pt_lo_done = sem("pt_filled"), sem("pt_hi_done"), sem("pt_lo_done")
        pv_filled, recip_done, y_done = sem("pv_filled"), sem("recip_done"), sem("y_done")
        v_filled, v1_done, v_full_done = sem("v_filled"), sem("v1_done"), sem("v_full_done")
        v_rest_done, v2_done, v3_done = sem("v_rest_done"), sem("v2_done"), sem("v3_done")
        yt_filled, yt_hi_done, yt_lo_done = sem("yt_filled"), sem("yt_hi_done"), sem("yt_lo_done")
        z_step, zt_done, zn_filled = sem("z_step"), sem("zt_done"), sem("zn_filled")
        ln1_step, ln1_rstd = sem("ln1_step"), sem("ln1_rstd")
        x1t_filled, x1t_done, x1t_hi_done, x1t_lo_done = (sem("x1t_filled"), sem("x1t_done"), sem("x1t_hi_done"),
                                                          sem("x1t_lo_done"))
        logit_filled, gate_step, gate_exp = sem("logit_filled"), sem("gate_step"), sem("gate_exp")
        ct_filled, ct_hi_done, ct_lo_done = sem("ct_filled"), sem("ct_hi_done"), sem("ct_lo_done")
        c_filled, c_done = sem("c_filled"), sem("c_done")
        up_filled, hid_done, hid_hi_done, hid_lo_done = (sem("up_filled"), sem("hid_done"), sem("hid_hi_done"),
                                                         sem("hid_lo_done"))
        down_step, col2_done, on_filled = sem("down_step"), sem("col2_done"), sem("on_filled")
        ln2_step, ln2_rstd = sem("ln2_step"), sem("ln2_rstd")

        def three_passes(dst, w_parts, m_parts, start=True, stop=True):
            for k, (a, b) in enumerate(((0, 0), (0, 1), (1, 0))):
                last = nc.tensor.matmul(dst, w_parts[a], m_parts[b], start=start and k == 0, stop=stop and k == 2)
            return last

        LN_STEPS = 1 + QT + QT + 1 + QT
        GATE_STEPS = 1 + QT + QT + 1 + 1 + TOP + 3 + TOP + 1

        def batch(eng, b, final, pair, tail):
            pair(b, 0, True, False, final)
            with eng.Fori(1, HP - 1) as i:
                pair(b, i, False, False, final)
            pair(b, HP - 1, False, True, final)
            tail(b, final)

        def all_batches(eng, pair, tail):
            with eng.Fori(0, B - 1) as b:
                batch(eng, b, False, pair, tail)
            batch(eng, B - 1, True, pair, tail)

        with nc.Block() as block:
            @block.sync
            def _(sp):
                def load_a(n, h, k):
                    sp.dma_start(a_st[:, k, :].bitcast(F32), a_dram[h]).then_inc(a_in[k], 16)

                sp.sem_inc(out_stored, 16)
                sp.dma_start(xt[:, 0, :, :].bitcast(F32), xt_dram[0]).then_inc(xt_in, 16)
                load_a(0, 0, 0)
                load_a(1, 1, 1)
                sp.dma_start(xt[:, 1, :, :].bitcast(F32), xt_dram[1]).then_inc(xt_in, 16)
                sp.dma_start(x_nat[:, :, :], x_tiles[0]).then_inc(x_in, 16)

                def pair(b, i, first, last, final):
                    n = b * H + i * 2
                    if not final:
                        sp.wait_ge(v_filled, b * 2 * QT + i + 2 * QT)
                        t = i // 2
                        sp.dma_start(xv[:, :, :].bitcast(F32), xt_dram[b + 1, :, :, bass.ds(t * P, P)]).then_inc(xv_in, 16)
                    for k in range(2):
                        if final and last:
                            continue
                        sp.wait_ge(g_filled, n + k + 1)
                        load_a(n + k + 2, (2 * i + k + 2) if not last else k, k)

                def tail(b, final):
                    if not final:
                        sp.wait_ge(s_filled, 3 * H * (b + 1))
                        sp.dma_start(xt[:, b % 2, :, :].bitcast(F32), xt_dram[(b + 2) % B]).then_inc(xt_in, 16)
                        sp.wait_ge(ln1_step, LN_STEPS * b + 1)
                        sp.dma_start(x_nat[:, :, :], x_tiles[b + 1]).then_inc(x_in, 16)
                    sp.wait_ge(ln2_step, LN_STEPS * (b + 1) + 1)
                    sp.dma_start(out_tiles[b], x2[:, :, :]).then_inc(out_stored, 16)

                all_batches(sp, pair, tail)
                sp.wait_ge(out_stored, 16 * (B + 1))
                sp.wait_ge(xt_in, 16 * (B + 1))

            @block.gpsimd
            def _(pool):
                pool.memset(zeros[:, :], 0.0).then_inc(const2, 1)
                pool.memset(v1[:, :, :, :, DV:VW], 1.0).then_inc(const2, 1)
                pool.wait_ge(const2, 2)

                def split_v(m, slot, t, half, wait=True):
                    hs = bass.ds(half * 8, 8)
                    if wait:
                        pool.wait_ge(v3_done, m)
                    pool.wait_ge(v_full_done, m + 1)
                    pool.tensor_tensor(v_rest[:, :].rearrange("p (h v) -> p h v", v=DV),
                                       v_full[:, :].rearrange("p (h v) -> p h v", v=DV),
                                       v1[:, slot, t, hs, 0:DV], ALU.subtract).then_inc(v_rest_done, 1)
                    pool.wait_ge(v_rest_done, m + 1)
                    pool.tensor_tensor(v2[:, slot, t, hs, :], v_rest[:, :].rearrange("p (h v) -> p h v", v=DV),
                                       zeros[:, :].rearrange("p (h v) -> p h v", v=DV), ALU.add).then_inc(v2_done, 1)
                    pool.wait_ge(v2_done, m + 1)
                    pool.tensor_tensor(v3[:, slot, t, hs, :], v_rest[:, :].rearrange("p (h v) -> p h v", v=DV),
                                       v2[:, slot, t, hs, :], ALU.subtract).then_inc(v3_done, 1)

                for u in range(2 * QT):
                    split_v(u, 0, u // 2, u % 2, u > 0)

                def pair(b, i, first, last, final):
                    if not final:
                        split_v(b * 2 * QT + i + 2 * QT, (b + 1) % 2, i // 2, i % 2)

                def tail(b, final):
                    pool.wait_ge(ln1_step, LN_STEPS * b + 2 + 2 * QT)
                    pool.tensor_tensor(rstd[:, :], eps_in[:, 0, :], eps_in[:, 1, :], ALU.pow).then_inc(ln1_rstd, 1)
                    for f in range(FT):
                        pool.wait_ge(hid_hi_done, FT * b + f + 1)
                        if f >= 3:
                            pool.wait_ge(down_step, FT * b + f - 2)
                        pool.tensor_tensor(act_lo[:, f % 3, :], hid[f % 3], act_hi[:, f % 3, :],
                                           ALU.subtract).then_inc(hid_lo_done, 1)
                    pool.wait_ge(ln2_step, LN_STEPS * b + 3 + 2 * QT)
                    pool.tensor_tensor(rstd[:, :], eps_in[:, 0, :], eps_in[:, 1, :], ALU.pow).then_inc(ln2_rstd, 1)

                all_batches(pool, pair, tail)

            @block.scalar
            def _(act):
                def v_unit(m, slot, t, half, bank):
                    hs = bass.ds(half * 8, 8)
                    act.wait_ge(v_filled, m + 1)
                    nc.scalar.activation(v1[:, slot, t, hs, 0:DV], bank.rearrange("p (h v) -> p h v", v=DV),
                                         ACT.Copy).then_inc(v1_done, 1)
                    act.wait_ge(v1_done, m + 1)

                def v_keep(m, bank, wait):
                    if wait:
                        act.wait_ge(v3_done, m)
                    nc.scalar.activation(v_full[:, :], bank, ACT.Copy).then_inc(v_full_done, 1)

                def g_high(n, k):
                    act.wait_ge(g_filled, n + 1)
                    nc.scalar.activation(g_hi[:, k, :], ps_g[:, :], ACT.Copy).then_inc(g_hi_done, 1)

                for k in range(2):
                    g_high(k, k)
                for u in range(2 * QT):
                    bank = ps_t[:, u % 2, :]
                    v_unit(u, 0, u // 2, u % 2, bank)
                    v_keep(u, bank, u > 0)

                def step(b, h, k, first, last, final, unit):
                    n = b * H + h
                    for i in range(QT):
                        act.wait_ge(max_done, n * QT + i + 1)
                        if i == 0 and not first:
                            act.wait_ge(pt_filled, 2 * n - 2)
                        w = (i + 1) * P
                        nc.scalar.activation(p[:, k, blk(i, 0) * P:blk(i, 0) * P + w],
                                             neg_s[:, k, blk(i, 0) * P:blk(i, 0) * P + w], ACT.Exp,
                                             bias=neg_max[:, k, i:i + 1], scale=-1.0).then_inc(exp_done, 1)
                    if unit is not None:
                        m, slot, t, half = unit
                        v_unit(m, slot, t, half, ps_g[:, :])
                        v_keep(m, ps_g[:, :], True)
                    if not first:
                        act.wait_ge(pv_filled, n - 1)
                    for c, (lo, hi) in enumerate(PT_PIECES):
                        act.wait_ge(pt_filled, 2 * n + c + 1)
                        nc.scalar.activation(pt_hi[:, k, lo * P:hi * P],
                                             ps_t[:, :, :].rearrange("p k c -> p (k c)")[:, lo * P:hi * P],
                                             ACT.Copy).then_inc(pt_hi_done, 1)
                    if not (final and last):
                        act.wait_ge(s_filled, 3 * n + 3)
                        g_high(n + 2, k)

                def pair(b, i, first, last, final):
                    step(b, 2 * i, 0, first, last, final, None)
                    unit = None if final else (b * 2 * QT + i + 2 * QT, (b + 1) % 2, i // 2, i % 2)
                    step(b, 2 * i + 1, 1, first, last, final, unit)

                def tail(b, final):
                    for c in range(HP):
                        act.wait_ge(yt_filled, HP * b + c + 1)
                        if c >= 2:
                            act.wait_ge(z_step, HP * b + c - 1)
                        nc.scalar.activation(act_hi[:, c % 2, :], ps_t[:, c % 2, :], ACT.Copy).then_inc(yt_hi_done, 1)
                    act.wait_ge(z_step, HP * (b + 1))
                    nc.scalar.activation(col[:, :], ps_t[:, 2, :], ACT.Copy).then_inc(zt_done, 1)
                    act.wait_ge(x1t_filled, b + 1)
                    nc.scalar.activation(x1t[:, :], ps_g[:, :], ACT.Copy).then_inc(x1t_done, 1)
                    act.wait_ge(gate_step, GATE_STEPS * b + 2 + 2 * QT)
                    nc.scalar.activation(gate[:, 1, :], gate[:, 0, :], ACT.Exp).then_inc(gate_exp, 1)
                    act.wait_ge(ct_filled, b + 1)
                    nc.scalar.activation(ct_hi[:, :], ps_y[0:E, :], ACT.Copy).then_inc(ct_hi_done, 1)
                    for f in range(FT):
                        e = f // FPE
                        if f % FPE == 0:
                            act.wait_ge(c_filled, E * b + e + 1)
                            if e >= 2:
                                act.wait_ge(hid_done, FT * b + (e - 1) * FPE)
                            nc.scalar.activation(c_row[e % 2], (ps_y if e % 2 else ps_g)[:, :],
                                                 ACT.Copy).then_inc(c_done, 1)
                        act.wait_ge(hid_done, FT * b + f + 1)
                        if f >= 3:
                            act.wait_ge(down_step, FT * b + f - 2)
                        nc.scalar.activation(act_hi[:, f % 3, :], hid[f % 3], ACT.Copy).then_inc(hid_hi_done, 1)
                    act.wait_ge(down_step, FT * (b + 1))
                    nc.scalar.activation(col[:, :], ps_t[:, 2, :], ACT.Copy).then_inc(col2_done, 1)

                all_batches(act, pair, tail)

            @block.vector
            def _(dve):
                def wait_apart(semaphore, value):
                    dve.wait_ge(semaphore, value)
                    dve.sem_inc(wait_carrier, 1)

                def g_low(n, k):
                    dve.wait_ge(g_hi_done, n + 1)
                    nc.vector.tensor_tensor(g_lo[:, k, :], ps_g[:, :], g_hi[:, k, :],
                                            ALU.subtract).then_inc(g_lo_done, 1)

                def row_max(n, k, guard):
                    for i in range(QT):
                        bank, at = S_AT[i]
                        w = (i + 1) * P
                        if i == 0 and guard is not None:
                            wait_apart(exp_done, guard)
                        if i != 1:
                            wait_apart(s_filled, 3 * n + max(i, 1))
                        nc.vector.tensor_tensor_reduce(
                            neg_s[:, k, blk(i, 0) * P:blk(i, 0) * P + w], ps_s[:, bank, at:at + w], mask[:, T - w:T],
                            -1.0, 3e38, ALU.add, ALU.min, neg_max[:, k, i:i + 1]).then_inc(max_done, 1)

                def norm(n, h):
                    ps = ps_y[:, 0:QT * VW].rearrange("p (t c) -> p t c", c=VW)
                    dve.wait_ge(pv_filled, n + 1)
                    nc.vector.reciprocal(r_sum[:, 0, :], ps[:, :, DV]).then_inc(recip_done, 1)
                    dve.wait_ge(recip_done, n + 1)
                    nc.vector.tensor_tensor(y[:, :, bass.ds(h * DV, DV)], ps[:, :, 0:DV],
                                            r_sum[:, 0, :].unsqueeze(2).to_broadcast([P, QT, DV]),
                                            ALU.mult).then_inc(y_done, 1)

                dve.sem_inc(ln2_step, 1)
                g_low(0, 0)
                row_max(0, 0, None)
                g_low(1, 1)

                def step(b, h, k, first, last, final):
                    n = b * H + h
                    done = final and last and k == 1
                    if not done:
                        row_max(n + 1, 1 - k, None if (first and k == 0) else n * QT)
                    for c, (lo, hi) in enumerate(PT_PIECES):
                        dve.wait_ge(pt_hi_done, 2 * n + c + 1)
                        nc.vector.tensor_tensor(pt_lo[:, k, lo * P:hi * P],
                                                ps_t[:, :, :].rearrange("p k c -> p (k c)")[:, lo * P:hi * P],
                                                pt_hi[:, k, lo * P:hi * P], ALU.subtract).then_inc(pt_lo_done, 1)
                    if not (final and last):
                        g_low(n + 2, k)
                    if not (first and k == 0):
                        norm(n - 1, h - 1)

                def pair(b, i, first, last, final):
                    step(b, 2 * i, 0, first, last, final)
                    step(b, 2 * i + 1, 1, first, last, final)

                def layer_norm(b, step_sem, rstd_sem, shortcut, dst, filled, guard):
                    c = LN_STEPS * b + (0 if dst is x1 else 1)
                    dve.wait_ge(filled, b + 1)
                    src = ps_g if dst is x1 else ps_y
                    nc.vector.tensor_tensor(res[:, :, :], src[:, :].rearrange("p (t d) -> p t d", d=D), shortcut,
                                            ALU.add).then_inc(step_sem, 1)
                    wait_apart(step_sem, c + 1)
                    for t in range(QT):
                        nc.vector.bn_stats(st[:, t, :], res[:, t, :]).then_inc(step_sem, 1)
                    wait_apart(step_sem, c + 1 + QT)
                    for t in range(QT):
                        nc.vector.bn_aggr(mv[:, t, :], st[:, t, :]).then_inc(step_sem, 1)
                    dve.wait_ge(step_sem, c + 1 + 2 * QT)
                    nc.vector.tensor_scalar(eps_in[:, 0, :], mv[:, :, 1], EPS, None, ALU.add).then_inc(step_sem, 1)
                    dve.wait_ge(rstd_sem, b + 1)
                    if guard is not None:
                        dve.wait_ge(*guard)
                    for t in range(QT):
                        nc.vector.tensor_scalar(dst[:, t, :], res[:, t, :], mv[:, t, 0:1], rstd[:, t:t + 1],
                                                ALU.subtract, ALU.mult).then_inc(step_sem, 1)

                def tail(b, final):
                    norm(b * H + H - 1, H - 1)
                    for c in range(HP):
                        dve.wait_ge(yt_hi_done, HP * b + c + 1)
                        nc.vector.tensor_tensor(act_lo[:, c % 2, :], ps_t[:, c % 2, :], act_hi[:, c % 2, :],
                                                ALU.subtract).then_inc(yt_lo_done, 1)
                    dve.wait_ge(x_in, 16 * (b + 1))
                    layer_norm(b, ln1_step, ln1_rstd, x_nat[:, :, :], x1, zn_filled, None)
                    dve.wait_ge(x1t_done, b + 1)
                    nc.vector.tensor_copy(x1t_hi[:, :], x1t[:, :]).then_inc(x1t_hi_done, 1)
                    dve.wait_ge(x1t_hi_done, b + 1)
                    nc.vector.tensor_tensor(x1t_lo[:, :], x1t[:, :], x1t_hi[:, :],
                                            ALU.subtract).then_inc(x1t_lo_done, 1)
                    g0 = GATE_STEPS * b
                    g = [g0]

                    def sync():
                        dve.wait_ge(gate_step, g[0])

                    def did(ins, count=1):
                        ins.then_inc(gate_step, 1)
                        g[0] = g[0] + 1

                    dve.wait_ge(logit_filled, b + 1)
                    did(nc.vector.tensor_copy(logit[:, :, :],
                                              ps_y[:, 0:QT * E].rearrange("p (t e) -> p t e", e=E)))
                    wait_apart(gate_step, g[0])
                    for t in range(QT):
                        did(nc.vector.max(best[:, t, :], logit[:, t, :]))
                    wait_apart(gate_step, g[0])
                    for t in range(QT):
                        did(nc.vector.max_index(best_at[:, t, :], best[:, t, :], logit[:, t, :]))
                    did(nc.vector.tensor_tensor(gate[:, 0, :], best[:, :, 1], best[:, :, 0], ALU.subtract))
                    sync()
                    did(nc.vector.tensor_copy(at_f[:, :, :], best_at[:, :, 0:TOP]))
                    sync()
                    for k in range(TOP):
                        did(nc.vector.tensor_tensor(pick[:, k, :, :], iota8[:, :, :],
                                                    at_f[:, :, k:k + 1].to_broadcast([P, QT, E]), ALU.is_equal))
                    dve.wait_ge(gate_exp, b + 1)
                    did(nc.vector.tensor_scalar(gate[:, 2, :], gate[:, 1, :], 1.0, None, ALU.add))
                    sync()
                    did(nc.vector.reciprocal(gate[:, 3, :], gate[:, 2, :]))
                    sync()
                    did(nc.vector.tensor_tensor(gate[:, 4, :], gate[:, 3, :], gate[:, 1, :], ALU.mult))
                    sync()
                    for k in range(TOP):
                        did(nc.vector.tensor_tensor(pick[:, k, :, :], pick[:, k, :, :],
                                                    gate[:, 3 + k, :].unsqueeze(2).to_broadcast([P, QT, E]),
                                                    ALU.mult))
                    sync()
                    did(nc.vector.tensor_tensor(comb[:, :, :], pick[:, 0, :, :], pick[:, 1, :, :], ALU.add))
                    dve.wait_ge(ct_hi_done, b + 1)
                    nc.vector.tensor_tensor(ct_lo[:, :], ps_y[0:E, :], ct_hi[:, :], ALU.subtract).then_inc(ct_lo_done, 1)
                    for f in range(FT):
                        e = f // FPE
                        dve.wait_ge(up_filled, FT * b + f + 1)
                        if f % FPE == 0:
                            dve.wait_ge(c_done, E * b + e + 1)
                        if f >= 3:
                            dve.wait_ge(hid_lo_done, FT * b + f - 2)
                        nc.vector.scalar_tensor_tensor(out=hid[f % 3], in0=ps_t[:, f % 2, :], scalar=0.0,
                                                       in1=c_row[e % 2], op0=ALU.max,
                                                       op1=ALU.mult).then_inc(hid_done, 1)
                    layer_norm(b, ln2_step, ln2_rstd, x1[:, :, :], x2, on_filled, (out_stored, (b + 1) * 16))

                all_batches(dve, pair, tail)

            @block.tensor
            def _(pe):
                def g_product(n, k, slot):
                    pe.wait_ge(a_in[k], ((n - k) // 2 + 1) * 16)
                    three_passes(ps_g[:, :], [a_st[:, k, q * P:(q + 1) * P] for q in range(2)],
                                 [xt[:, slot, q, :] for q in range(2)]).then_inc(g_filled, 1)

                def scores(n, k, slot, guard):
                    pe.wait_ge(g_lo_done, n + 1)
                    for i in range(QT):
                        bank, at = S_AT[i]
                        if guard is not None and i != 1:
                            pe.wait_ge(max_done, guard + max(i + 1, 2))
                        ins = three_passes(ps_s[:, bank, at:at + S_COLS[i]],
                                           [g[:, k, i * P:(i + 1) * P] for g in (g_hi, g_lo)],
                                           [xt[:, slot, q, 0:S_COLS[i]] for q in range(2)])
                        if i:
                            ins.then_inc(s_filled, 1)

                def p_transpose(n, k, first):
                    for i in range(QT):
                        pe.wait_ge(exp_done, n * QT + i + 1)
                        for j in range(i + 1):
                            m = blk(i, j)
                            if not first and m == 0:
                                pe.wait_ge(pt_lo_done, 2 * n - 1)
                            if not first and m == 4:
                                pe.wait_ge(pt_lo_done, 2 * n)
                            ins = nc.tensor.transpose(ps_t[:, m // 4, (m % 4) * P:(m % 4 + 1) * P],
                                                      p[:, k, m * P:(m + 1) * P], ident[:, :])
                            if m == 3 or m == NBLK - 1:
                                ins.then_inc(pt_filled, 1)

                def pv(n, h, k, slot):
                    pe.wait_ge(pt_lo_done, 2 * n + 2)
                    for i in range(QT):
                        at = i * VW
                        for j in range(i + 1):
                            m = slice(blk(i, j) * P, (blk(i, j) + 1) * P)
                            o, o1 = ps_y[:, at:at + DV], ps_y[:, at:at + VW]
                            nc.tensor.matmul(o1, pt_hi[:, k, m], v1[:, slot, j, h, :], start=j == 0, stop=False)
                            nc.tensor.matmul(o, pt_hi[:, k, m], v2[:, slot, j, h, :], start=False, stop=False)
                            nc.tensor.matmul(o, pt_hi[:, k, m], v3[:, slot, j, h, :], start=False, stop=False)
                            nc.tensor.matmul(o, pt_lo[:, k, m], v2[:, slot, j, h, :], start=False, stop=False)
                            ins = nc.tensor.matmul(o1, pt_lo[:, k, m], v1[:, slot, j, h, :], start=False, stop=j == i)
                    ins.then_inc(pv_filled, 1)

                def v_product(w_parts, half, dst):
                    return three_passes(dst, w_parts, [vt[:, q, bass.ds(half * BANK, BANK)] for q in range(2)])

                pe.wait_ge(xt_in, 16)
                g_product(0, 0, 0)
                pe.wait_ge(g_lo_done, 1)
                g_product(1, 1, 0)
                scores(0, 0, 0, None)
                for u in range(2 * QT):
                    if u >= 2:
                        pe.wait_ge(v_full_done, u - 1)
                    t = u // 2
                    v_product([xt[:, 0, q, t * P:(t + 1) * P] for q in range(2)], u % 2,
                              ps_t[:, u % 2, :]).then_inc(v_filled, 1)
                pe.wait_ge(v_full_done, 2 * QT)

                def step(b, h, k, first, last, final, i):
                    n = b * H + h
                    edge = last and k == 1
                    slot = b % 2
                    if not (edge and final):
                        if edge:
                            pe.wait_ge(xt_in, (b + 2) * 16)
                        scores(n + 1, 1 - k, (b + 1) % 2 if edge else slot, n * QT)
                    if k == 1 and not final:
                        m = b * 2 * QT + i + 2 * QT
                        pe.wait_ge(xv_in, (m - 2 * QT + 1) * 16)
                        v_product([xv[:, q, :] for q in range(2)], i % 2, ps_g[:, :]).then_inc(v_filled, 1)
                    p_transpose(n, k, first and k == 0)
                    if not (last and final):
                        if k == 1 and not final:
                            pe.wait_ge(v_full_done, m + 1)
                        else:
                            pe.wait_ge(g_lo_done, n + 2)
                        if last and k == 0:
                            pe.wait_ge(xt_in, (b + 2) * 16)
                        g_product(n + 2, k, (b + 1) % 2 if last else slot)
                    if not (first and k == 0):
                        if first:
                            pe.wait_ge(v3_done, (b + 1) * 2 * QT)
                            pe.wait_ge(ln2_step, b * LN_STEPS + 1)
                        else:
                            pe.wait_ge(y_done, n - 1)
                        pv(n - 1, h - 1, 1 - k, slot)

                def pair(b, i, first, last, final):
                    step(b, 2 * i, 0, first, last, final, i)
                    step(b, 2 * i + 1, 1, first, last, final, i)

                def tail(b, final):
                    n = b * H + H - 1
                    pe.wait_ge(y_done, n)
                    pv(n, H - 1, 1, b % 2)
                    for c in range(HP + 1):
                        if c < HP:
                            if c == 0:
                                pe.wait_ge(y_done, n + 1)
                            if c >= 2:
                                pe.wait_ge(yt_lo_done, HP * b + c - 1)
                            for t in range(QT):
                                ins = nc.tensor.transpose(ps_t[:, c % 2, t * P:(t + 1) * P],
                                                          y[:, t, c * P:(c + 1) * P], ident[:, :])
                            ins.then_inc(yt_filled, 1)
                        if c >= 1:
                            q = c - 1
                            pe.wait_ge(yt_lo_done, HP * b + q + 1)
                            three_passes(ps_t[:, 2, :], [wc[:, s, q * P:(q + 1) * P] for s in range(2)],
                                         [a[:, q % 2, :] for a in (act_hi, act_lo)], start=q == 0,
                                         stop=q == HP - 1).then_inc(z_step, 1)
                    pe.wait_ge(zt_done, b + 1)
                    if not final:
                        pe.wait_ge(g_lo_done, (b + 1) * H + 2)
                    for t in range(QT):
                        ins = nc.tensor.transpose(ps_g[:, t * P:(t + 1) * P], col[:, t * P:(t + 1) * P], ident[:, :])
                    ins.then_inc(zn_filled, 1)
                    pe.wait_ge(ln1_step, LN_STEPS * (b + 1))
                    for t in range(QT):
                        ins = nc.tensor.transpose(ps_g[:, t * P:(t + 1) * P], x1[:, t, :], ident[:, :])
                    ins.then_inc(x1t_filled, 1)
                    pe.wait_ge(x1t_done, b + 1)
                    for t in range(QT):
                        ins = nc.tensor.matmul(ps_y[:, t * E:(t + 1) * E], x1t[:, t * P:(t + 1) * P], wg[:, :],
                                               start=True, stop=True)
                    ins.then_inc(logit_filled, 1)
                    pe.wait_ge(x1t_lo_done, b + 1)

                    def up(f):
                        if f >= 2:
                            pe.wait_ge(hid_done, FT * b + f - 1)
                        three_passes(ps_t[:, f % 2, :], [w1[:, s, f * P:(f + 1) * P] for s in range(2)],
                                     [x1t_hi[:, :], x1t_lo[:, :]]).then_inc(up_filled, 1)

                    def weights_row(e):
                        if e >= 2:
                            pe.wait_ge(c_done, E * b + e - 1)
                        dst = (ps_y if e % 2 else ps_g)[:, :]
                        nc.tensor.matmul(dst, sel[:, e * P:(e + 1) * P], ct_hi[:, :], start=True, stop=False)
                        nc.tensor.matmul(dst, sel[:, e * P:(e + 1) * P], ct_lo[:, :], start=False,
                                         stop=True).then_inc(c_filled, 1)

                    up(0)
                    up(1)
                    pe.wait_ge(gate_step, GATE_STEPS * (b + 1))
                    for t in range(QT):
                        ins = nc.tensor.transpose(ps_y[0:E, t * P:(t + 1) * P], comb[:, t, :], ident[:, :])
                    ins.then_inc(ct_filled, 1)
                    pe.wait_ge(ct_lo_done, b + 1)
                    weights_row(0)
                    weights_row(1)
                    for f in range(FT + 3):
                        if 2 <= f < FT:
                            up(f)
                            if f % FPE == 0 and f // FPE + 1 < E:
                                weights_row(f // FPE + 1)
                        if f >= 3:
                            q = f - 3
                            pe.wait_ge(hid_lo_done, FT * b + q + 1)
                            three_passes(ps_t[:, 2, :], [w2[:, s, q * P:(q + 1) * P] for s in range(2)],
                                         [a[:, q % 3, :] for a in (act_hi, act_lo)], start=q == 0,
                                         stop=q == FT - 1).then_inc(down_step, 1)
                    pe.wait_ge(col2_done, b + 1)
                    for t in range(QT):
                        ins = nc.tensor.transpose(ps_y[:, t * P:(t + 1) * P], col[:, t * P:(t + 1) * P], ident[:, :])
                    ins.then_inc(on_filled, 1)

                all_batches(pe, pair, tail)


_INS = ['L0_attn_x', 'L0_attn_Q', 'L0_attn_K', 'L0_attn_V', 'L0_attn_W', 'L0_ffn_Wg', 'L0_ffn_W1', 'L0_ffn_W2']
_OUTS = [((4, 512, 128), 'float32')]


def kernel(**inputs):
    import numpy as _np
    import concourse.bacc as _bacc
    from concourse import mybir as _mybir
    from concourse.bass_utils import run_bass_kernel_spmd as _run

    nc = _bacc.Bacc("TRN2", target_bir_lowering=False, num_devices=1)
    arrays, args = {}, []
    for name in _INS:
        a = _np.ascontiguousarray(inputs[name])
        arrays[f"in_{name}_dram"] = a
        args.append(nc.dram_tensor(f"in_{name}_dram", a.shape, _mybir.dt.from_np(a.dtype), kind="ExternalInput").ap())
    for i, (shape, dtype) in enumerate(_OUTS):
        dt = _mybir.dt.from_np(_np.dtype(dtype))
        args.append(nc.dram_tensor(f"out_{i}_dram", shape, dt, kind="ExternalOutput").ap())
    post_ln_layer(nc, *args)
    r = _run(nc, [arrays], core_ids=[0])
    got = tuple(r.results[0][f"out_{i}_dram"] for i in range(len(_OUTS)))
    return got[0]
```

```python
from contextlib import ExitStack

import concourse.bass as bass
from concourse import mybir

F32 = mybir.dt.float32
F32R = mybir.dt.float32r
F16 = mybir.dt.float16
BF16 = mybir.dt.bfloat16
U32 = mybir.dt.uint32
ALU = mybir.AluOpType
ACT = mybir.ActivationFunctionType

P = 128
BANK = 512
EPS = 1e-5
MASKED = -1e30


def post_ln_layer(nc, x, Q, K, V, W, Wg, W1, W2, out):
    B, T, D = x.shape
    DQ, _, H = Q.shape
    DV = V.shape[0]
    E, _, F = W1.shape
    QT = T // P
    HP = H // 2
    FT = E * F // P
    FPE = F // P
    TOP = 2
    NBLK = QT * (QT + 1) // 2
    VW = DV + 2
    UNITS = 2 * QT
    POOL_FIRST = [2, 5]
    DVE_FIRST = [u for u in range(UNITS) if u not in POOL_FIRST]
    ROTATE, PREP_X1T, PREP_GATE, PREP_ROWS, OUT_AT = 6, 6, 9, 13, 3
    LAG = 3
    RING = 4
    QK_SCALE = (DQ / D) / DQ
    Z_SCALE = 1.0 / H
    assert D == P and T == BANK and DQ == DV == 64 and E == 8 and HP == UNITS

    WCH = E * F // HP

    def blk(i, j):
        return i * (i + 1) // 2 + j

    S_PIECE = [0, 0, 1, 2]
    S_AT = [0, 256, 0, 0]
    S_COLS = [256, 256, 384, 512]
    PIECES = 3
    PT_PIECES = [(0, 4), (4, NBLK)]

    a_dram = nc.dram_tensor("a_parts", (H, P, 2 * P), F32).ap()
    xt_dram = nc.dram_tensor("xt_parts", (B, P, 2, T), F32).ap()

    x_tiles = x.rearrange("b (t p) d -> b p t d", p=P)
    out_tiles = out.rearrange("b (t p) d -> b p t d", p=P)

    with ExitStack() as ctx:
        def sb(name, shape, dt, c=ctx):
            return c.enter_context(nc.sbuf_tensor(name, shape, dt))

        def sem(name):
            return ctx.enter_context(nc.semaphore(name))

        ps_s = ctx.enter_context(nc.psum_tensor("ps_s", [P, 2, BANK], F32))
        ps_t = ctx.enter_context(nc.psum_tensor("ps_t", [P, 3, BANK], F32))
        ps_g = ctx.enter_context(nc.psum_tensor("ps_g", [P, BANK], F32))
        ps_y = ctx.enter_context(nc.psum_tensor("ps_y", [P, BANK], F32))
        ps_z = ctx.enter_context(nc.psum_tensor("ps_z", [P, BANK], F32))

        ident = sb("ident", [P, P], F32)
        mask = sb("mask", [P, T], F32)
        iota8 = sb("iota8", [P, QT, E], F32)
        eps_in = sb("eps_in", [P, 2, QT], F32)
        wg = sb("wg", [P, E], F32)
        vt = sb("vt", [P, 2, H * DV], F32R)
        wc = sb("wc", [P, 2, HP * D], F32R)
        w1 = sb("w1", [P, 2, E * F], F32R)
        w2 = sb("w2", [P, 2, FT * D], F32R)
        w_raw1 = sb("w_raw1", [P, E * F], F32)
        a_st = sb("a_st", [P, 2, 2 * P], F32R)
        xt = sb("xt", [P, 2, 2, T], F32R)

        in_q, in_k, in_v, in_w, in_w1, in_w2, in_wg = [
            sem(f"loaded_{n}") for n in ("q", "k", "v", "w", "w1", "w2", "wg")]
        in_x = [sem(f"loaded_x{b}") for b in range(B)]
        const_step = sem("const_step")
        setup_filled = sem("setup_filled")
        setup_hi = sem("setup_hi")
        setup_lo = sem("setup_lo")
        w_hi = sem("w_hi")
        w_lo = sem("w_lo")
        w_sorted = sem("w_sorted")
        xt_out = sem("xt_out")
        a_out = sem("a_out")
        a_in = [sem(f"a_in_{k}") for k in range(2)]

        with ExitStack() as sctx:
            x_raw = sb("x_raw", [P, B * QT, D], F32, sctx)
            q_raw = sb("q_raw", [DQ, D * H], F32, sctx)
            k_raw = sb("k_raw", [DQ, D * H], F32, sctx)
            v_raw = sb("v_raw", [DV, D * H], F32, sctx)
            w_raw = sb("w_raw", [D, DV * H], F32, sctx)
            w_h = sb("w_h", [D, H * DV], F32, sctx)
            a_all = sb("a_all", [P, H, 2, P], F32R, sctx)
            xt_rest = sb("xt_rest", [P, B - 2, 2, T], F32R, sctx)

            q_h = q_raw[:, :].rearrange("q (d h) -> q h d", h=H)
            k_h = k_raw[:, :].rearrange("q (d h) -> q h d", h=H)
            v_h = v_raw[:, :].rearrange("v (d h) -> v h d", h=H)

            def setup_bank(k):
                return [ps_s[:, 0, :], ps_s[:, 1, :], ps_t[:, 0, :], ps_t[:, 1, :], ps_t[:, 2, :], ps_g[:, :],
                        ps_y[:, :], ps_z[:, :]][k % 8]

            jobs = [("x", 0), ("x", 1), ("a", 0)] + [("v", i) for i in range(2)] + \
                   [("a", q) for q in range(1, H // 4)] + [("x", b) for b in range(2, B)] + \
                   [("w", i) for i in range(2)]

            def done_by(kind, n):
                return jobs.index((kind, n)) + 1

            def job_out(kind, n, part):
                if kind == "x":
                    return (xt[:, n, part, :] if n < 2 else xt_rest[:, n - 2, part, :]), 1.0
                if kind == "a":
                    return a_all[:, 4 * n:4 * n + 4, part, :], QK_SCALE
                if kind == "v":
                    return vt[:, part, n * BANK:(n + 1) * BANK], 1.0
                return wc[:, part, n * BANK:(n + 1) * BANK], Z_SCALE

            def job_in(k, kind):
                bank = setup_bank(k)
                return bank.rearrange("p (h d) -> p h d", h=4) if kind == "a" else bank

            with nc.Block() as block:
                @block.sync
                def _(sp):
                    for b in range(B):
                        sp.dma_start(x_raw[:, b * QT:(b + 1) * QT, :], x_tiles[b]).then_inc(in_x[b], 16)
                    sp.dma_start(v_raw[:, :], V.rearrange("v d h -> v (d h)")).then_inc(in_v, 16)
                    sp.dma_start(w_raw1[:, :].rearrange("d (e f) -> d e f", e=E),
                                 W1.rearrange("e d f -> d e f")).then_inc(in_w1, 16)
                    sp.wait_ge(setup_lo, done_by("a", 0))
                    for k in range(2):
                        sp.dma_start(a_st[:, k, :].bitcast(F32),
                                     a_all[:, k, :, :].bitcast(F32).rearrange("p k c -> p (k c)")).then_inc(a_in[k], 16)
                    sp.wait_ge(setup_lo, done_by("a", H // 4 - 1))
                    sp.dma_start(a_dram.rearrange("h p c -> p h c"),
                                 a_all[:, :, :, :].bitcast(F32).rearrange("p h k c -> p h (k c)")).then_inc(a_out, 16)
                    sp.wait_ge(setup_lo, done_by("x", B - 1))
                    sp.dma_start(xt_dram[2:B].rearrange("b p k t -> p b k t"),
                                 xt_rest[:, :, :, :].bitcast(F32)).then_inc(xt_out, 16)
                    sp.wait_ge(a_out, 16)
                    sp.wait_ge(xt_out, 16)

                @block.gpsimd
                def _(pool):
                    pool.memset(ident[:, :], 0.0).then_inc(const_step, 1)
                    pool.wait_ge(const_step, 1)
                    pool.affine_select(out=ident[:, :], in_=ident[:, :], compare_op=ALU.not_equal, fill=1.0, base=0,
                                       pattern=[[-1, P]], channel_multiplier=1).then_inc(const_step, 1)
                    pool.memset(mask[:, :], 0.0).then_inc(const_step, 1)
                    pool.memset(eps_in[:, 1, :], -0.5).then_inc(const_step, 1)
                    pool.iota(iota8[:, :, :], pattern=[[0, QT], [1, E]], base=0, channel_multiplier=0,
                              allow_small_or_imprecise_dtypes=True).then_inc(const_step, 1)
                    pool.wait_ge(const_step, 3)
                    pool.affine_select(out=mask[:, T - P:T], in_=mask[:, T - P:T], compare_op=ALU.is_ge, fill=MASKED,
                                       base=0, pattern=[[-1, P]], channel_multiplier=1).then_inc(const_step, 1)

                @block.scalar
                def _(act):
                    act.dma_start(q_raw[:, :], Q.rearrange("q d h -> q (d h)")).then_inc(in_q, 16)
                    act.dma_start(k_raw[:, :], K.rearrange("q d h -> q (d h)")).then_inc(in_k, 16)
                    act.dma_start(w_raw[:, :], W.rearrange("d v h -> d (v h)")).then_inc(in_w, 16)
                    act.dma_start(wg[:, :], Wg).then_inc(in_wg, 16)
                    for k, (kind, n) in enumerate(jobs):
                        act.wait_ge(setup_filled, k + 1)
                        dst, scale = job_out(kind, n, 0)
                        nc.scalar.activation(dst, job_in(k, kind), ACT.Copy, scale=scale).then_inc(setup_hi, 1)

                @block.vector
                def _(dve):
                    for k, (kind, n) in enumerate(jobs):
                        if kind == "w" and n == 0:
                            dve.wait_ge(in_w, 16)
                            nc.vector.tensor_copy(w_h[:, :].rearrange("d (h v) -> d h v", h=H),
                                                  w_raw[:, :].rearrange("d (v h) -> d h v", h=H)).then_inc(w_sorted, 1)
                        dve.wait_ge(setup_hi, k + 1)
                        dst, scale = job_out(kind, n, 1)
                        nc.vector.scalar_tensor_tensor(out=dst, in0=job_in(k, kind), scalar=scale,
                                                       in1=job_out(kind, n, 0)[0], op0=ALU.mult,
                                                       op1=ALU.subtract).then_inc(setup_lo, 1)

                @block.tensor
                def _(pe):
                    pe.wait_ge(const_step, 2)
                    for k, (kind, n) in enumerate(jobs):
                        if k >= 8:
                            pe.wait_ge(setup_lo, k - 7)
                        bank = setup_bank(k)
                        if kind == "x":
                            pe.wait_ge(in_x[n], 16)
                            for t in range(QT):
                                last = nc.tensor.transpose(bank[:, t * P:(t + 1) * P], x_raw[:, n * QT + t, :],
                                                           ident[:, :])
                        elif kind == "a":
                            if n == 0:
                                pe.wait_ge(in_q, 16)
                                pe.wait_ge(in_k, 16)
                            for h in range(4):
                                last = nc.tensor.matmul(bank[:, h * P:(h + 1) * P], q_h[:, 4 * n + h, :],
                                                        k_h[:, 4 * n + h, :], start=True, stop=True)
                        elif kind == "v":
                            if n == 0:
                                pe.wait_ge(in_v, 16)
                            for h in range(8):
                                last = nc.tensor.transpose(bank[:, h * DV:(h + 1) * DV], v_h[:, 8 * n + h, :],
                                                           ident[0:DV, 0:DV])
                        else:
                            pe.wait_ge(w_sorted, 1)
                            for c in range(4):
                                last = nc.tensor.transpose(bank[:, c * P:(c + 1) * P],
                                                           w_h[:, (4 * n + c) * P:(4 * n + c + 1) * P], ident[:, :])
                        last.then_inc(setup_filled, 1)

        xv = sb("xv", [P, 2, P], F32R)
        x_nat = sb("x_nat", [P, QT, D], F32)
        w_raw2 = sb("w_raw2", [P, FT * D], F32)
        sel_raw = sb("sel_raw", [2 * E, E * P], F32)
        sel = sb("sel", [2 * E, E * P], F32R)
        ct = sb("ct", [2 * E, T], F32R)
        comb_parts = sb("comb_parts", [P, QT, 2 * E], F32R)
        v1 = sb("v1", [P, 2, QT, H, VW], BF16)
        v2 = sb("v2", [P, 2, QT, H, DV], BF16)
        v3 = sb("v3", [P, 2, QT, H, DV], BF16)
        v_full = sb("v_full", [P, BANK], F32)
        v_rest = sb("v_rest", [P, 2, BANK], F32)
        zeros = sb("zeros", [P, BANK], F32)
        zeros_b = zeros[:, :].bitcast(BF16)
        wz = sb("wz", [P, 2, P], F32R)
        g_hi = sb("g_hi", [P, 2, T], F32R)
        g_lo = sb("g_lo", [P, 2, T], F32R)
        p = sb("p", [P, 2, NBLK * P], F32)
        neg_max = sb("neg_max", [P, 2, QT], F32)
        pt_hi = sb("pt_hi", [P, 2, NBLK * P], F16)
        pt_lo = sb("pt_lo", [P, 2, NBLK * P], F16)
        y = sb("y", [P, QT, 2 * DV], F32)
        r_sum = sb("r_sum", [P, QT], F32)
        yt_hi = sb("yt_hi", [P, T], F32R)
        yt_lo = sb("yt_lo", [P, T], F32R)
        col = sb("col", [P, T], F32)
        res = sb("res", [P, QT, D], F32)
        x1 = sb("x1", [P, B, QT, D], F32)
        st = sb("st", [P, QT, 6], F32)
        mv = sb("mv", [P, QT, 2], F32)
        rstd = sb("rstd", [P, QT], F32)
        logit = sb("logit", [P, QT, E], F32)
        best = sb("best", [P, QT, E], F32)
        best_at = sb("best_at", [P, QT, E], U32)
        at_f = sb("at_f", [P, QT, TOP], F32)
        gate = sb("gate", [P, 5, QT], F32)
        pick = sb("pick", [P, 2, QT, E], F32)
        comb = sb("comb", [P, QT, E], F32)
        p_flat = p[:, :, :].rearrange("p k c -> p (k c)")
        hid = [p_flat[:, i * BANK:(i + 1) * BANK] for i in range(RING)]
        c_row = [p_flat[:, RING * BANK:(RING + 1) * BANK], v_rest[:, 1, :]]
        hid_hi = [g_hi[:, 0, :], g_hi[:, 1, :], yt_hi[:, :], vt[:, 0, 0:BANK]]
        hid_lo = [g_lo[:, 0, :], g_lo[:, 1, :], yt_lo[:, :], vt[:, 1, 0:BANK]]
        up_bank = [ps_t[:, 0, :], ps_t[:, 1, :], ps_t[:, 2, :], ps_s[:, 1, :]]
        row_bank = ps_s[:, 0, :]
        x1t = v_full
        x1_fix = v_rest[:, 0, :]
        x1t_parts = xt
        x2 = x_nat

        xt_in = sem("xt_in")
        xv_in = sem("xv_in")
        x_in = sem("x_in")
        wz_in = sem("wz_in")
        x1_in = sem("x1_in")
        out_stored = sem("out_stored")
        const2 = sem("const2")
        wait_carrier = sem("wait_carrier")
        g_filled, g_hi_done, g_lo_done = sem("g_filled"), sem("g_hi_done"), sem("g_lo_done")
        s_filled, max_done, exp_done = sem("s_filled"), sem("max_done"), sem("exp_done")
        pt_filled, pt_hi_done, pt_lo_done = sem("pt_filled"), sem("pt_hi_done"), sem("pt_lo_done")
        pv_filled, recip_done, y_done = sem("pv_filled"), sem("recip_done"), sem("y_done")
        v_filled, v1_done, v_full_done = sem("v_filled"), sem("v1_done"), sem("v_full_done")
        v_rest_done, v2_done, v3_done = sem("v_rest_done"), sem("v2_done"), sem("v3_done")
        v_first_step = sem("v_first_step")
        yt_filled, yt_hi_done, yt_lo_done = sem("yt_filled"), sem("yt_hi_done"), sem("yt_lo_done")
        z_step, zt_done, zn_filled, zn_taken = sem("z_step"), sem("zt_done"), sem("zn_filled"), sem("zn_taken")
        ln1_step, ln1_rstd = sem("ln1_step"), sem("ln1_rstd")
        x1t_filled, x1t_done, x1t_hi_done, x1t_lo_done = (sem("x1t_filled"), sem("x1t_done"), sem("x1t_hi_done"),
                                                          sem("x1t_lo_done"))
        logit_filled, gate_step, gate_exp = sem("logit_filled"), sem("gate_step"), sem("gate_exp")
        ct_filled, ct_done = sem("ct_filled"), sem("ct_done")
        sel_step = sem("sel_step")
        c_filled, c_done = sem("c_filled"), sem("c_done")
        up_filled, hid_done, hid_hi_done, hid_lo_done = (sem("up_filled"), sem("hid_done"), sem("hid_hi_done"),
                                                         sem("hid_lo_done"))
        down_step, col2_done, on_filled = sem("down_step"), sem("col2_done"), sem("on_filled")
        ln2_step, ln2_rstd, on_taken = sem("ln2_step"), sem("ln2_rstd"), sem("on_taken")

        def three_passes(dst, w_parts, m_parts, start=True, stop=True):
            for k, (a, b) in enumerate(((0, 0), (0, 1), (1, 0))):
                last = nc.tensor.matmul(dst, w_parts[a], m_parts[b], start=start and k == 0, stop=stop and k == 2)
            return last

        LN_STEPS = 1 + QT + QT + 1 + QT
        Z_STEPS = HP + 1
        GATE_STEPS = 1 + QT + QT + 1 + 1 + TOP + 3 + TOP + 3

        def attention(eng, start, pair, first_pair, end):
            start()
            with eng.Fori(0, B - 1) as b:
                with eng.Fori(1, HP - 1) as i:
                    pair(b, i, False, False)
                pair(b, HP - 1, True, False)
                first_pair(b)
            with eng.Fori(1, HP - 1) as i:
                pair(B - 1, i, False, True)
            pair(B - 1, HP - 1, True, True)
            end()

        def experts(eng, stage):
            for s in range(ROTATE):
                stage(0, s, False)
            with eng.Fori(0, B - 1) as b:
                for s in range(ROTATE, FT + ROTATE):
                    stage(b, s, False)
            for s in range(ROTATE, FT + OUT_AT):
                stage(B - 1, s, True)

        with nc.Block() as block:
            @block.sync
            def _(sp):
                sp.sem_inc(out_stored, 16)
                sp.dma_start(w_raw2[:, :].rearrange("f (c d) -> f c d", d=D),
                             W2.rearrange("e (c f) d -> f (e c) d", f=P)).then_inc(in_w2, 16)

                def load_a(n, k, head):
                    sp.wait_ge(g_filled, n + 1)
                    sp.dma_start(a_st[:, k, :].bitcast(F32), a_dram[head]).then_inc(a_in[k], 16)

                def load_wz(b, c):
                    sp.wait_ge(z_step, Z_STEPS * b + c + 1)
                    sp.dma_start(wz[:, :, :].bitcast(F32),
                                 wc[:, :, bass.ds(c * P, P)].bitcast(F32)).then_inc(wz_in, 16)

                def load_xv(b, j):
                    sp.wait_ge(v_filled, b * UNITS + j + UNITS)
                    sp.dma_start(xv[:, :, :].bitcast(F32),
                                 xt[:, (b + 1) % 2, :, bass.ds(j // 2 * P, P)].bitcast(F32)).then_inc(xv_in, 16)

                def start():
                    sp.sem_inc(xt_in, 16)
                    for k in range(2):
                        load_a(k, k, 2 + k)
                    for k in range(2):
                        load_a(2 + k, k, 4 + k)

                def pair(b, i, last, final):
                    n = b * H + i * 2
                    if not final:
                        sp.wait_ge(xt_in, (b + 1) * 16)
                        load_xv(b, i - 1)
                    load_wz(b, i - 1)
                    if last:
                        sp.wait_ge(zn_taken, b + 1)
                        sp.dma_start(x_nat[:, :, :], x_tiles[b]).then_inc(x_in, 16)
                    if not (final and last):
                        for k in range(2):
                            load_a(n + k + 2, k, (2 * i + k + 4) % H)

                def first_pair(b):
                    n = (b + 1) * H
                    sp.wait_ge(s_filled, PIECES * n)
                    sp.dma_start(xt[:, b % 2, :, :].bitcast(F32), xt_dram[b % 2 + 2]).then_inc(xt_in, 16)
                    load_xv(b, UNITS - 1)
                    load_wz(b, HP - 1)
                    for k in range(2):
                        load_a(n + k + 2, k, k + 4)

                def stage_x1(b):
                    sp.wait_ge(ln1_step, LN_STEPS * (b + 1))
                    sp.dma_start(x1_fix, x1[:, b, :, :].rearrange("p t d -> p (t d)")).then_inc(x1_in, 16)

                def end():
                    sp.wait_ge(v3_done, (B - 1) * UNITS + len(POOL_FIRST))
                    stage_x1(0)
                    load_wz(B - 1, HP - 1)

                attention(sp, start, pair, first_pair, end)

                def stage(b, s, final):
                    if s == PREP_X1T and not final:
                        sp.wait_ge(x1t_filled, b + 1)
                        stage_x1(b + 1)
                    if s == FT + OUT_AT - final:
                        sp.wait_ge(ln2_step, LN_STEPS * (b + 1) + 1)
                        sp.dma_start(out_tiles[b], x2[:, :, :]).then_inc(out_stored, 16)

                experts(sp, stage)
                sp.wait_ge(out_stored, 16 * (B + 1))
                sp.wait_ge(xt_in, 16 * B)
                for k in range(2):
                    sp.wait_ge(a_in[k], 16 * (B * HP + 1))

            @block.gpsimd
            def _(pool):
                pool.memset(zeros[:, :], 0.0).then_inc(const2, 1)
                pool.memset(v1[:, :, :, :, DV:VW], 1.0).then_inc(const2, 1)
                pool.memset(sel_raw[:, :], 0.0).then_inc(sel_step, 1)
                for r in range(2):
                    pool.wait_ge(sel_step, r + 1)
                    pool.affine_select(out=sel_raw[:, :].rearrange("p (e c) -> p e c", e=E),
                                       in_=sel_raw[:, :].rearrange("p (e c) -> p e c", e=E),
                                       compare_op=ALU.not_equal, fill=1.0, base=-r * E, pattern=[[-1, E], [0, P]],
                                       channel_multiplier=1).then_inc(sel_step, 1)
                pool.wait_ge(const2, 2)

                def split_v(m, s, slot, t, half, guard=True):
                    hs = bass.ds(half * 8, 8)
                    rest = v_rest[:, 0, :].rearrange("p (h v) -> p h v", v=DV)
                    if guard:
                        pool.wait_ge(v3_done, s)
                    pool.wait_ge(v_full_done, s + 1)
                    pool.tensor_tensor(rest, v_full[:, :].rearrange("p (h v) -> p h v", v=DV),
                                       v1[:, slot, t, hs, 0:DV], ALU.subtract).then_inc(v_rest_done, 1)
                    pool.wait_ge(v_rest_done, s + 1)
                    pool.tensor_tensor(v2[:, slot, t, hs, :], rest,
                                       zeros[:, :].rearrange("p (h v) -> p h v", v=DV), ALU.add).then_inc(v2_done, 1)
                    pool.wait_ge(v2_done, s + 1)
                    pool.tensor_tensor(v3[:, slot, t, hs, :], rest, v2[:, slot, t, hs, :],
                                       ALU.subtract).then_inc(v3_done, 1)

                def start():
                    for s, u in enumerate(POOL_FIRST):
                        split_v(u, s, 0, u // 2, u % 2, s > 0)

                def split_w(c):
                    at = bass.ds(c * WCH, WCH)
                    for q, (w, raw) in enumerate(((w1, w_raw1), (w2, w_raw2))):
                        pool.wait_ge(w_hi, 2 * c + q + 1)
                        pool.tensor_tensor(w[:, 1, at], raw[:, at], w[:, 0, at], ALU.subtract).then_inc(w_lo, 1)

                def pair(b, i, last, final):
                    if not final:
                        split_v(None, b * UNITS + i - 1 + len(POOL_FIRST), (b + 1) % 2, (i - 1) // 2, (i - 1) % 2)
                    else:
                        split_w(i - 1)
                        if last:
                            split_w(i)

                def rstd_of(step_sem, rstd_sem, b):
                    pool.wait_ge(step_sem, LN_STEPS * b + 2 + 2 * QT + (1 if step_sem is ln2_step else 0))
                    pool.tensor_tensor(rstd[:, :], eps_in[:, 0, :], eps_in[:, 1, :], ALU.pow).then_inc(rstd_sem, 1)

                def first_pair(b):
                    split_v(None, b * UNITS + UNITS - 1 + len(POOL_FIRST), (b + 1) % 2, (UNITS - 1) // 2, 1)
                    rstd_of(ln1_step, ln1_rstd, b)

                attention(pool, start, pair, first_pair, lambda: rstd_of(ln1_step, ln1_rstd, B - 1))

                def stage(b, s, final):
                    if s < FT or not final:
                        pool.wait_ge(hid_hi_done, FT * b + s + 1)
                        if not isinstance(b, int) or b > 0 or s >= RING:
                            pool.wait_ge(down_step, FT * b + s - RING + 1)
                        pool.tensor_tensor(hid_lo[s % RING], hid[s % RING], hid_hi[s % RING],
                                           ALU.subtract).then_inc(hid_lo_done, 1)
                    if s == FT + OUT_AT - final:
                        rstd_of(ln2_step, ln2_rstd, b)

                experts(pool, stage)

            @block.scalar
            def _(act):
                def v_high(m, s, slot, t, half, bank, wait):
                    hs = bass.ds(half * 8, 8)
                    act.wait_ge(v_filled, m + 1)
                    nc.scalar.activation(v1[:, slot, t, hs, 0:DV], bank.rearrange("p (h v) -> p h v", v=DV),
                                         ACT.Copy).then_inc(v1_done, 1)
                    if s is not None:
                        act.wait_ge(v1_done, m + 1)
                        if wait:
                            act.wait_ge(v3_done, s)
                        nc.scalar.activation(v_full[:, :], bank, ACT.Copy).then_inc(v_full_done, 1)

                def g_high(n, k):
                    act.wait_ge(g_filled, n + 1)
                    nc.scalar.activation(g_hi[:, k, :], ps_g[:, :], ACT.Copy).then_inc(g_hi_done, 1)

                def yt_high(b, c, bank):
                    act.wait_ge(yt_filled, b * HP + c + 1)
                    act.wait_ge(z_step, Z_STEPS * b + c + 1)
                    nc.scalar.activation(yt_hi[:, :], bank, ACT.Copy).then_inc(yt_hi_done, 1)

                def start():
                    for k in range(2):
                        g_high(k, k)
                    act.wait_ge(const2, 2)
                    for u in range(UNITS):
                        s = POOL_FIRST.index(u) if u in POOL_FIRST else None
                        v_high(u, s, 0, u // 2, u % 2, ps_t[:, u % 3, :], s != 0)
                    for k in range(2):
                        step(k, k, k)
                    act.wait_ge(sel_step, 3)
                    nc.scalar.activation(sel[:, :], sel_raw[:, :], ACT.Copy).then_inc(sel_step, 1)

                def split_w(c):
                    at = bass.ds(c * WCH, WCH)
                    for w, raw, raw_in in ((w1, w_raw1, in_w1), (w2, w_raw2, in_w2)):
                        act.wait_ge(raw_in, 16)
                        nc.scalar.activation(w[:, 0, at], raw[:, at], ACT.Copy).then_inc(w_hi, 1)

                def step(n, k, static_n=None, unit=None, split=None, chunk=None, z_of=None, ahead=True):
                    for q in range(QT):
                        act.wait_ge(max_done, n * QT + q + 1)
                        at = slice(blk(q, 0) * P, (blk(q, q) + 1) * P)
                        nc.scalar.activation(p[:, k, at], p[:, k, at], ACT.Exp, bias=neg_max[:, k, q:q + 1],
                                             scale=-1.0).then_inc(exp_done, 1)
                    if ahead:
                        act.wait_ge(s_filled, PIECES * (n + 1))
                        g_high(n + 2, k)
                    if static_n is None:
                        act.wait_ge(pv_filled, n - 1)
                    for c, (lo, hi) in enumerate(PT_PIECES):
                        act.wait_ge(pt_filled, 2 * n + c + 1)
                        nc.scalar.activation(pt_hi[:, k, lo * P:hi * P],
                                             ps_t[:, :, :].rearrange("p k c -> p (k c)")[:, lo * P:hi * P],
                                             ACT.Copy).then_inc(pt_hi_done, 1)
                    if chunk is not None:
                        yt_high(*chunk, ps_g[:, :])
                    if z_of is not None:
                        act.wait_ge(z_step, Z_STEPS * (z_of + 1))
                        nc.scalar.activation(col[:, :], ps_z[:, :], ACT.Copy).then_inc(zt_done, 1)
                    if unit is not None:
                        b, j = unit
                        v_high(b * UNITS + j + UNITS, b * UNITS + j + len(POOL_FIRST), (b + 1) % 2, j // 2, j % 2,
                               ps_g[:, :], True)
                    if split is not None:
                        split_w(split)

                def pair(b, i, last, final):
                    n = b * H + 2 * i
                    ahead = not (last and final)
                    step(n, 0, unit=None if final else (b, i - 1), split=i - 1 if final else None, ahead=ahead)
                    step(n + 1, 1, chunk=(b, i - 1), split=i if final and last else None, ahead=ahead)

                def first_pair(b):
                    n = (b + 1) * H
                    step(n, 0, unit=(b, UNITS - 1))
                    step(n + 1, 1, chunk=(b, HP - 1), z_of=b)

                def take_x1t(b):
                    act.wait_ge(x1t_filled, b + 1)
                    nc.scalar.activation(x1t[:, :], ps_g[:, :], ACT.Copy).then_inc(x1t_done, 1)

                def gate_part(b):
                    act.wait_ge(gate_step, GATE_STEPS * b + 2 + 2 * QT)
                    nc.scalar.activation(gate[:, 1, :], gate[:, 0, :], ACT.Exp).then_inc(gate_exp, 1)

                def take_ct(b):
                    act.wait_ge(ct_filled, b + 1)
                    nc.scalar.activation(ct[:, :], ps_y[0:2 * E, :], ACT.Copy).then_inc(ct_done, 1)

                def end():
                    act.wait_ge(v3_done, (B - 1) * UNITS + len(POOL_FIRST))
                    take_x1t(0)
                    yt_high(B - 1, HP - 1, row_bank)
                    act.wait_ge(z_step, Z_STEPS * B)
                    nc.scalar.activation(col[:, :], ps_z[:, :], ACT.Copy).then_inc(zt_done, 1)
                    gate_part(0)
                    take_ct(0)

                attention(act, start, pair, first_pair, end)

                def take_row(b, e):
                    act.wait_ge(c_filled, E * b + e + 1)
                    if not isinstance(b, int) or b > 0 or e >= 2:
                        act.wait_ge(hid_done, FT * b + (e - 1) * FPE)
                    nc.scalar.activation(c_row[e % 2], row_bank, ACT.Copy).then_inc(c_done, 1)

                def stage(b, s, final):
                    if s < FT or not final:
                        if s == 0:
                            take_row(b, 0)
                        if s % FPE == 1 and (s + 1 < FT or not final):
                            take_row(b, (s + 1) // FPE)
                        act.wait_ge(hid_done, FT * b + s + 1)
                        if not isinstance(b, int) or b > 0 or s >= RING:
                            act.wait_ge(down_step, FT * b + s - RING + 1)
                        nc.scalar.activation(hid_hi[s % RING], hid[s % RING], ACT.Copy).then_inc(hid_hi_done, 1)
                    if not final and s == PREP_X1T:
                        take_x1t(b + 1)
                    if not final and s == PREP_GATE:
                        gate_part(b + 1)
                    if not final and s == PREP_ROWS:
                        take_ct(b + 1)
                    if s == FT + OUT_AT - 1:
                        act.wait_ge(down_step, FT * (b + 1))
                        nc.scalar.activation(col[:, :], ps_z[:, :], ACT.Copy).then_inc(col2_done, 1)

                experts(act, stage)

            @block.vector
            def _(dve):
                def wait_apart(semaphore, value):
                    dve.wait_ge(semaphore, value)
                    dve.sem_inc(wait_carrier, 1)

                def g_low(n, k):
                    dve.wait_ge(g_hi_done, n + 1)
                    nc.vector.tensor_tensor(g_lo[:, k, :], ps_g[:, :], g_hi[:, k, :],
                                            ALU.subtract).then_inc(g_lo_done, 1)

                def row_max(n, k, q, guard=None):
                    if q == 0 and guard is not None:
                        wait_apart(pt_filled, guard)
                    if q != 1:
                        wait_apart(s_filled, PIECES * n + S_PIECE[q] + 1)
                    w = (q + 1) * P
                    nc.vector.tensor_tensor_reduce(
                        p[:, k, blk(q, 0) * P:(blk(q, q) + 1) * P],
                        ps_s[:, (k + S_PIECE[q]) % 2, S_AT[q]:S_AT[q] + w], mask[:, T - w:T], -1.0, 3e38, ALU.add,
                        ALU.min, neg_max[:, k, q:q + 1]).then_inc(max_done, 1)

                def norm(n, k):
                    ps = ps_y[:, 0:QT * VW].rearrange("p (t c) -> p t c", c=VW)
                    dve.wait_ge(pv_filled, n + 1)
                    nc.vector.reciprocal(r_sum[:, :], ps[:, :, DV]).then_inc(recip_done, 1)
                    dve.wait_ge(recip_done, n + 1)
                    nc.vector.tensor_tensor(y[:, :, k * DV:(k + 1) * DV], ps[:, :, 0:DV],
                                            r_sum[:, :].unsqueeze(2).to_broadcast([P, QT, DV]),
                                            ALU.mult).then_inc(y_done, 1)

                def pt_low(n, k, c):
                    lo, hi = PT_PIECES[c]
                    dve.wait_ge(pt_hi_done, 2 * n + c + 1)
                    nc.vector.tensor_tensor(pt_lo[:, k, lo * P:hi * P],
                                            ps_t[:, :, :].rearrange("p k c -> p (k c)")[:, lo * P:hi * P],
                                            pt_hi[:, k, lo * P:hi * P], ALU.subtract).then_inc(pt_lo_done, 1)

                def yt_low(m, bank):
                    dve.wait_ge(yt_hi_done, m + 1)
                    nc.vector.tensor_tensor(yt_lo[:, :], bank, yt_hi[:, :], ALU.subtract).then_inc(yt_lo_done, 1)

                dve.sem_inc(ln2_step, 1)
                dve.sem_inc(zn_taken, 1)
                dve.sem_inc(on_taken, 1)

                def start():
                    g_low(0, 0)
                    for q in range(QT):
                        row_max(0, 0, q)
                    g_low(1, 1)
                    first_v()
                    step(0, 0, free=True, norm_before=False)
                    step(1, 1)

                def first_v():
                    for s, u in enumerate(DVE_FIRST):
                        rest = v_rest[:, 1, :].rearrange("p (h v) -> p h v", v=DV)
                        at = (slice(None), 0, u // 2, slice(u % 2 * 8, u % 2 * 8 + 8))
                        dve.wait_ge(v1_done, u + 1)
                        nc.vector.tensor_tensor(rest, ps_t[:, u % 3, :].rearrange("p (h v) -> p h v", v=DV),
                                                v1[(*at, slice(0, DV))], ALU.subtract).then_inc(v_first_step, 1)
                        dve.wait_ge(v_first_step, 3 * s + 1)
                        nc.vector.tensor_copy(v2[at], rest).then_inc(v_first_step, 1)
                        dve.wait_ge(v_first_step, 3 * s + 2)
                        nc.vector.tensor_tensor(v3[at], rest, v2[at], ALU.subtract).then_inc(v_first_step, 1)
                        dve.wait_ge(v_first_step, 3 * s + 3)

                def step(n, k, free=False, chunk=None, z_of=None, more=True, ahead=True, norm_before=True):
                    if more:
                        for q in range(QT - 1):
                            row_max(n + 1, 1 - k, q, None if free else 2 * n)
                    if ahead:
                        g_low(n + 2, k)
                    pt_low(n, k, 0)
                    if more:
                        row_max(n + 1, 1 - k, QT - 1)
                    pt_low(n, k, 1)
                    if chunk is not None:
                        yt_low(chunk, ps_g[:, :])
                    if norm_before:
                        norm(n - 1, 1 - k)

                def pair(b, i, last, final):
                    n = b * H + 2 * i
                    ahead = not (last and final)
                    step(n, 0, ahead=ahead)
                    step(n + 1, 1, chunk=b * HP + i - 1, more=ahead, ahead=ahead)

                def moments(c, b, step_sem, src, shortcut, filled, taken):
                    dve.wait_ge(filled, b + 1)
                    nc.vector.tensor_tensor(res[:, :, :], src.rearrange("p (t d) -> p t d", d=D), shortcut,
                                            ALU.add).then_inc(step_sem, 1)
                    wait_apart(step_sem, c + 1)
                    dve.sem_inc(taken, 1)
                    for t in range(QT):
                        nc.vector.bn_stats(st[:, t, :], res[:, t, :]).then_inc(step_sem, 1)
                    wait_apart(step_sem, c + 1 + QT)
                    for t in range(QT):
                        nc.vector.bn_aggr(mv[:, t, :], st[:, t, :]).then_inc(step_sem, 1)
                    dve.wait_ge(step_sem, c + 1 + 2 * QT)
                    nc.vector.tensor_scalar(eps_in[:, 0, :], mv[:, :, 1], EPS, None, ALU.add).then_inc(step_sem, 1)

                def normalise(b, step_sem, rstd_sem, dst, guard):
                    dve.wait_ge(rstd_sem, b + 1)
                    if guard is not None:
                        dve.wait_ge(*guard)
                    for t in range(QT):
                        nc.vector.tensor_scalar(dst[:, t, :], res[:, t, :], mv[:, t, 0:1], rstd[:, t:t + 1],
                                                ALU.subtract, ALU.mult).then_inc(step_sem, 1)

                def first_norm(b):
                    dve.wait_ge(x_in, 16 * (b + 1))
                    moments(LN_STEPS * b, b, ln1_step, ps_g[:, :], x_nat[:, :, :], zn_filled, zn_taken)
                    normalise(b, ln1_step, ln1_rstd, x1[:, b, :, :], None)

                def first_pair(b):
                    n = (b + 1) * H
                    step(n, 0)
                    step(n + 1, 1, chunk=b * HP + HP - 1)
                    first_norm(b)

                def split_x1t(b):
                    slot = b % 2
                    dve.wait_ge(x1t_done, b + 1)
                    nc.vector.tensor_copy(x1t_parts[:, slot, 0, :], x1t[:, :]).then_inc(x1t_hi_done, 1)
                    dve.wait_ge(x1t_hi_done, b + 1)
                    nc.vector.tensor_tensor(x1t_parts[:, slot, 1, :], x1t[:, :], x1t_parts[:, slot, 0, :],
                                            ALU.subtract).then_inc(x1t_lo_done, 1)

                def choose(b):
                    g = [GATE_STEPS * b]

                    def sync():
                        dve.wait_ge(gate_step, g[0])

                    def did(ins):
                        ins.then_inc(gate_step, 1)
                        g[0] = g[0] + 1

                    dve.wait_ge(logit_filled, b + 1)
                    did(nc.vector.tensor_copy(logit[:, :, :],
                                              ps_y[:, 0:QT * E].rearrange("p (t e) -> p t e", e=E)))
                    wait_apart(gate_step, g[0])
                    for t in range(QT):
                        did(nc.vector.max(best[:, t, :], logit[:, t, :]))
                    wait_apart(gate_step, g[0])
                    for t in range(QT):
                        did(nc.vector.max_index(best_at[:, t, :], best[:, t, :], logit[:, t, :]))
                    did(nc.vector.tensor_tensor(gate[:, 0, :], best[:, :, 1], best[:, :, 0], ALU.subtract))
                    sync()
                    did(nc.vector.tensor_copy(at_f[:, :, :], best_at[:, :, 0:TOP]))
                    sync()
                    for k in range(TOP):
                        did(nc.vector.tensor_tensor(pick[:, k, :, :], iota8[:, :, :],
                                                    at_f[:, :, k:k + 1].to_broadcast([P, QT, E]), ALU.is_equal))
                    dve.wait_ge(gate_exp, b + 1)
                    did(nc.vector.tensor_scalar(gate[:, 2, :], gate[:, 1, :], 1.0, None, ALU.add))
                    sync()
                    did(nc.vector.reciprocal(gate[:, 3, :], gate[:, 2, :]))
                    sync()
                    did(nc.vector.tensor_tensor(gate[:, 4, :], gate[:, 3, :], gate[:, 1, :], ALU.mult))
                    sync()
                    for k in range(TOP):
                        did(nc.vector.tensor_tensor(pick[:, k, :, :], pick[:, k, :, :],
                                                    gate[:, 3 + k, :].unsqueeze(2).to_broadcast([P, QT, E]),
                                                    ALU.mult))
                    sync()
                    did(nc.vector.tensor_tensor(comb[:, :, :], pick[:, 0, :, :], pick[:, 1, :, :], ALU.add))
                    sync()
                    did(nc.vector.tensor_copy(comb_parts[:, :, 0:E], comb[:, :, :]))
                    sync()
                    did(nc.vector.tensor_tensor(comb_parts[:, :, E:2 * E], comb[:, :, :], comb_parts[:, :, 0:E],
                                                ALU.subtract))

                def end():
                    norm(B * H - 1, 1)
                    dve.wait_ge(xt_in, 16 * B)
                    split_x1t(0)
                    yt_low(B * HP - 1, row_bank)
                    choose(0)
                    first_norm(B - 1)

                attention(dve, start, pair, first_pair, end)

                def stage(b, s, final):
                    if s < FT or not final:
                        dve.wait_ge(up_filled, FT * b + s + 1)
                        if s % FPE == 0:
                            dve.wait_ge(c_done, E * b + s // FPE + 1)
                        if not isinstance(b, int) or b > 0 or s >= RING:
                            dve.wait_ge(hid_lo_done, FT * b + s - RING + 1)
                        nc.vector.scalar_tensor_tensor(out=hid[s % RING], in0=up_bank[s % RING], scalar=0.0,
                                                       in1=c_row[s // FPE % 2], op0=ALU.max,
                                                       op1=ALU.mult).then_inc(hid_done, 1)
                    if not final and s == PREP_X1T:
                        split_x1t(b + 1)
                    if not final and s == PREP_GATE:
                        choose(b + 1)
                    if s == FT + OUT_AT - final:
                        moments(LN_STEPS * b + 1, b, ln2_step, ps_g[:, :], x1[:, b, :, :], on_filled, on_taken)
                    if s == FT + OUT_AT + 1 or (final and s == FT + OUT_AT - 1):
                        normalise(b, ln2_step, ln2_rstd, x2[:, :, :], (out_stored, (b + 1) * 16))

                experts(dve, stage)

            @block.tensor
            def _(pe):
                def g_product(n, k, slot):
                    pe.wait_ge(a_in[k], ((n - k) // 2 + 1) * 16)
                    three_passes(ps_g[:, :], [a_st[:, k, q * P:(q + 1) * P] for q in range(2)],
                                 [xt[:, slot, q, :] for q in range(2)]).then_inc(g_filled, 1)

                def scores(n, k, slot, piece, guard):
                    if guard is not None:
                        pe.wait_ge(max_done, guard)
                    for q in range(QT):
                        if S_PIECE[q] == piece:
                            ins = three_passes(ps_s[:, (k + piece) % 2, S_AT[q]:S_AT[q] + S_COLS[q]],
                                               [g[:, k, q * P:(q + 1) * P] for g in (g_hi, g_lo)],
                                               [xt[:, slot, c, 0:S_COLS[q]] for c in range(2)])
                    ins.then_inc(s_filled, 1)

                def p_transpose(n, k, q, first):
                    pe.wait_ge(exp_done, n * QT + q + 1)
                    for j in range(q + 1):
                        m = blk(q, j)
                        if not first and m == 0:
                            pe.wait_ge(pt_lo_done, 2 * n - 1)
                        if not first and m == 4:
                            pe.wait_ge(pt_lo_done, 2 * n)
                        ins = nc.tensor.transpose(ps_t[:, m // 4, (m % 4) * P:(m % 4 + 1) * P],
                                                  p[:, k, m * P:(m + 1) * P], ident[:, :])
                        if m == 3 or m == NBLK - 1:
                            ins.then_inc(pt_filled, 1)

                def pv(n, h, k, slot):
                    pe.wait_ge(pt_lo_done, 2 * n + 2)
                    for q in range(QT):
                        o, o1 = ps_y[:, q * VW:q * VW + DV], ps_y[:, q * VW:(q + 1) * VW]
                        for j in range(q + 1):
                            m = slice(blk(q, j) * P, (blk(q, j) + 1) * P)
                            nc.tensor.matmul(o1, pt_hi[:, k, m], v1[:, slot, j, h, :], start=j == 0, stop=False)
                            nc.tensor.matmul(o, pt_hi[:, k, m], v2[:, slot, j, h, :], start=False, stop=False)
                            nc.tensor.matmul(o, pt_hi[:, k, m], v3[:, slot, j, h, :], start=False, stop=False)
                            ins = nc.tensor.matmul(o1, pt_lo[:, k, m], v1[:, slot, j, h, :], start=False, stop=j == q)
                    ins.then_inc(pv_filled, 1)

                def yt_chunk(m, bank):
                    pe.wait_ge(y_done, 2 * m + 2)
                    for t in range(QT):
                        ins = nc.tensor.transpose(bank[:, t * P:(t + 1) * P], y[:, t, :], ident[:, :])
                    ins.then_inc(yt_filled, 1)

                def open_z():
                    nc.tensor.matmul(ps_z[:, :], zeros_b[:, 0:P], zeros_b[:, 0:T], start=True,
                                     stop=False).then_inc(z_step, 1)

                def z_product(m, last):
                    pe.wait_ge(wz_in, (m + 1) * 16)
                    pe.wait_ge(yt_lo_done, m + 1)
                    three_passes(ps_z[:, :], [wz[:, q, :] for q in range(2)], [yt_hi[:, :], yt_lo[:, :]],
                                 start=False, stop=last).then_inc(z_step, 1)

                pe.wait_ge(const2, 2)
                open_z()
                g_product(0, 0, 0)
                pe.wait_ge(g_lo_done, 1)
                g_product(1, 1, 0)
                scores(0, 0, 0, 0, None)
                scores(0, 0, 0, 1, None)
                for u in range(UNITS):
                    if u == 1:
                        scores(0, 0, 0, 2, 2)
                    if u >= 3:
                        if u - 3 in POOL_FIRST:
                            pe.wait_ge(v_full_done, POOL_FIRST.index(u - 3) + 1)
                        else:
                            pe.wait_ge(v_first_step, 3 * DVE_FIRST.index(u - 3) + 1)
                    t = u // 2
                    three_passes(ps_t[:, u % 3, :], [xt[:, 0, q, t * P:(t + 1) * P] for q in range(2)],
                                 [vt[:, q, u % 2 * BANK:(u % 2 + 1) * BANK] for q in range(2)]).then_inc(v_filled, 1)
                pe.wait_ge(v_full_done, len(POOL_FIRST))
                pe.wait_ge(v_first_step, 3 * len(DVE_FIRST))

                def step(n, k, h, slot, next_slot=None, ahead_slot=None, before=True, before_slot=None, v_guard=None,
                         unit=None, chunk=None, z_end=None, free_g=None, static_n=None):
                    if ahead_slot is not None:
                        pe.wait_ge(g_lo_done, n + 2)
                        if free_g is not None:
                            pe.wait_ge(v_full_done, free_g)
                        g_product(n + 2, k, ahead_slot)
                    if next_slot is not None:
                        pe.wait_ge(g_lo_done, n + 2)
                        scores(n + 1, 1 - k, next_slot, 0, n * QT + 3)
                        scores(n + 1, 1 - k, next_slot, 1, n * QT + 4)
                    for q in range(QT - 1):
                        p_transpose(n, k, q, static_n == 0)
                    if next_slot is not None:
                        scores(n + 1, 1 - k, next_slot, 2, (n + 1) * QT + 2)
                    p_transpose(n, k, QT - 1, static_n == 0)
                    if ahead_slot is not None and (unit is not None or chunk is not None):
                        pe.wait_ge(g_lo_done, n + 3)
                    if unit is not None:
                        b, j = unit
                        pe.wait_ge(xv_in, (b * UNITS + j + 1) * 16)
                        three_passes(ps_g[:, :], [xv[:, q, :] for q in range(2)],
                                     [vt[:, q, bass.ds(j % 2 * BANK, BANK)] for q in range(2)]).then_inc(v_filled, 1)
                    if chunk is not None:
                        yt_chunk(chunk, ps_g)
                    if before:
                        if v_guard is not None:
                            pe.wait_ge(v3_done, v_guard)
                        if static_n is None:
                            pe.wait_ge(y_done, n - 1)
                        pv(n - 1, h - 1, 1 - k, slot if before_slot is None else before_slot)
                    if chunk is not None:
                        z_product(chunk, z_end is not None)
                    if z_end is not None:
                        natural_z(z_end)
                        open_z()

                def natural_z(b):
                    pe.wait_ge(zt_done, b + 1)
                    for t in range(QT):
                        ins = nc.tensor.transpose(ps_g[:, t * P:(t + 1) * P], col[:, t * P:(t + 1) * P], ident[:, :])
                    ins.then_inc(zn_filled, 1)

                def start():
                    step(0, 0, 0, 0, next_slot=0, ahead_slot=0, before=False, static_n=0)
                    step(1, 1, 1, 0, next_slot=0, ahead_slot=0, v_guard=len(POOL_FIRST), static_n=1)

                def v_split(b, j):
                    return b * UNITS + j + len(POOL_FIRST) + 1

                def pair(b, i, last, final):
                    n = b * H + 2 * i
                    slot, other = b % 2, (b + 1) % 2
                    if last and not final:
                        pe.wait_ge(xt_in, (b + 1) * 16)
                    ahead = (None if final else other) if last else slot
                    step(n, 0, 2 * i, slot, next_slot=slot, ahead_slot=ahead, unit=None if final else (b, i - 1))
                    step(n + 1, 1, 2 * i + 1, slot, next_slot=ahead, ahead_slot=ahead,
                         free_g=None if final else v_split(b, i - 1), chunk=b * HP + i - 1)

                def first_pair(b):
                    n = (b + 1) * H
                    slot, other = b % 2, (b + 1) % 2
                    step(n, 0, H, other, next_slot=other, ahead_slot=other, before_slot=slot, unit=(b, UNITS - 1))
                    step(n + 1, 1, 1, other, next_slot=other, ahead_slot=other, free_g=v_split(b, UNITS - 1),
                         v_guard=(b + 1) * UNITS + len(POOL_FIRST), chunk=(b + 1) * HP - 1, z_end=b)
                    pe.wait_ge(zn_taken, b + 2)

                def x1_transpose(b):
                    pe.wait_ge(x1_in, 16 * (b + 1))
                    for t in range(QT):
                        ins = nc.tensor.transpose(ps_g[:, t * P:(t + 1) * P], x1_fix[:, t * P:(t + 1) * P],
                                                  ident[:, :])
                    ins.then_inc(x1t_filled, 1)

                def logits(b):
                    pe.wait_ge(x1t_done, b + 1)
                    for t in range(QT):
                        ins = nc.tensor.matmul(ps_y[:, t * E:(t + 1) * E], x1t[:, t * P:(t + 1) * P], wg[:, :],
                                               start=True, stop=True)
                    ins.then_inc(logit_filled, 1)

                def comb_transpose(b):
                    pe.wait_ge(gate_step, GATE_STEPS * (b + 1))
                    for t in range(QT):
                        ins = nc.tensor.transpose(ps_y[0:2 * E, t * P:(t + 1) * P],
                                                  comb_parts[:, t, :].bitcast(F32), ident[:, :])
                    ins.then_inc(ct_filled, 1)

                def end():
                    n = B * H - 1
                    x1_transpose(0)
                    pe.wait_ge(y_done, n)
                    pv(n, H - 1, 1, (B - 1) % 2)
                    yt_chunk(B * HP - 1, row_bank)
                    pe.wait_ge(in_wg, 16)
                    logits(0)
                    z_product(B * HP - 1, True)
                    natural_z(B - 1)
                    comb_transpose(0)

                attention(pe, start, pair, first_pair, end)

                def up(b, s):
                    if s % FT == 0:
                        pe.wait_ge(x1t_lo_done, b + s // FT + 1)
                    if not isinstance(b, int) or b > 0 or s >= RING:
                        pe.wait_ge(hid_done, FT * b + s - RING + 1)
                    f = s % FT
                    three_passes(up_bank[s % RING], [w1[:, c, f * P:(f + 1) * P] for c in range(2)],
                                 [x1t_parts[:, (b + s // FT) % 2, c, :] for c in range(2)]).then_inc(up_filled, 1)

                def weights_row(b, e):
                    if e % E == 0:
                        pe.wait_ge(ct_done, b + e // E + 1)
                    if not isinstance(b, int) or b > 0 or e >= 1:
                        pe.wait_ge(c_done, E * b + e)
                    else:
                        pe.wait_ge(yt_lo_done, B * HP)
                    nc.tensor.matmul(row_bank, sel[:, e % E * P:(e % E + 1) * P], ct[:, :], start=True,
                                     stop=True).then_inc(c_filled, 1)

                def down(b, s):
                    pe.wait_ge(hid_lo_done, FT * b + s + 1)
                    if s == FT:
                        pe.wait_ge(col2_done, b + 1)
                    f = s % FT
                    three_passes(ps_z[:, :], [w2[:, c, f * P:(f + 1) * P] for c in range(2)],
                                 [hid_hi[s % RING], hid_lo[s % RING]], start=f == 0,
                                 stop=f == FT - 1).then_inc(down_step, 1)

                def stage(b, s, final):
                    if s < FT or not final:
                        up(b, s)
                        if s == 0:
                            weights_row(b, 0)
                        if s % FPE == 1 and (s + 1 < FT or not final):
                            weights_row(b, (s + 1) // FPE)
                    if s >= LAG:
                        down(b, s - LAG)
                    if not final and s == PREP_X1T:
                        pe.wait_ge(zn_taken, B + 1)
                        pe.wait_ge(on_taken, b + 1)
                        x1_transpose(b + 1)
                    if not final and s == PREP_X1T + 1:
                        logits(b + 1)
                    if not final and s == PREP_ROWS:
                        comb_transpose(b + 1)
                    if s == FT + OUT_AT - final:
                        pe.wait_ge(col2_done, b + 1)
                        for t in range(QT):
                            ins = nc.tensor.transpose(ps_g[:, t * P:(t + 1) * P], col[:, t * P:(t + 1) * P],
                                                      ident[:, :])
                        ins.then_inc(on_filled, 1)

                pe.wait_ge(w_lo, 2 * HP)
                pe.wait_ge(sel_step, 4)
                experts(pe, stage)


_INS = ['L0_attn_x', 'L0_attn_Q', 'L0_attn_K', 'L0_attn_V', 'L0_attn_W', 'L0_ffn_Wg', 'L0_ffn_W1', 'L0_ffn_W2']
_OUTS = [((4, 512, 128), 'float32')]


def kernel(**inputs):
    import numpy as _np
    import concourse.bacc as _bacc
    from concourse import mybir as _mybir
    from concourse.bass_utils import run_bass_kernel_spmd as _run

    nc = _bacc.Bacc("TRN2", target_bir_lowering=False, num_devices=1)
    arrays, args = {}, []
    for name in _INS:
        a = _np.ascontiguousarray(inputs[name])
        arrays[f"in_{name}_dram"] = a
        args.append(nc.dram_tensor(f"in_{name}_dram", a.shape, _mybir.dt.from_np(a.dtype), kind="ExternalInput").ap())
    for i, (shape, dtype) in enumerate(_OUTS):
        dt = _mybir.dt.from_np(_np.dtype(dtype))
        args.append(nc.dram_tensor(f"out_{i}_dram", shape, dt, kind="ExternalOutput").ap())
    post_ln_layer(nc, *args)
    r = _run(nc, [arrays], core_ids=[0])
    got = tuple(r.results[0][f"out_{i}_dram"] for i in range(len(_OUTS)))
    return got[0]
```

```python
from contextlib import ExitStack

import concourse.bass as bass
from concourse import mybir

F32 = mybir.dt.float32
F32R = mybir.dt.float32r
F16 = mybir.dt.float16
BF16 = mybir.dt.bfloat16
U32 = mybir.dt.uint32
ALU = mybir.AluOpType
ACT = mybir.ActivationFunctionType

P = 128
BANK = 512
EPS = 1e-5
MASKED = -1e30


def post_ln_layer(nc, x, Q, K, V, W, Wg, W1, W2, out):
    B, T, D = x.shape
    DQ, _, H = Q.shape
    DV = V.shape[0]
    E, _, F = W1.shape
    QT = T // P
    HP = H // 2
    FT = E * F // P
    FPE = F // P
    TOP = 2
    NBLK = QT * (QT + 1) // 2
    VW = DV + 2
    UNITS = 2 * QT
    ROTATE, PREP_X1T, PREP_GATE, PREP_ROWS, OUT_AT = 6, 6, 9, 13, 3
    LAG = 3
    RING = 4
    QK_SCALE = (DQ / D) / DQ
    P_SCALE = 2.0 ** 15
    Z_SCALE = 1.0 / H
    assert D == P and T == BANK and DQ == DV == 64 and E == HP == UNITS == 8 and FPE == 2

    def blk(i, j):
        return i * (i + 1) // 2 + j

    S_PIECE = [0, 0, 1, 2]
    S_AT = [0, 256, 0, 0]
    S_COLS = [256, 256, 384, 512]
    PIECES = 3
    PT_PIECES = [(0, 4), (4, NBLK)]

    a_dram = nc.dram_tensor("a_parts", (H, P, 2 * P), F32).ap()
    xt_dram = nc.dram_tensor("xt_parts", (B, P, 2, T), F32).ap()

    x_tiles = x.rearrange("b (t p) d -> b p t d", p=P)
    w2_tiles = W2.rearrange("e (c f) d -> e f c d", f=P)
    out_tiles = out.rearrange("b (t p) d -> b p t d", p=P)

    with ExitStack() as ctx:
        def sb(name, shape, dt, c=ctx):
            return c.enter_context(nc.sbuf_tensor(name, shape, dt))

        def sem(name):
            return ctx.enter_context(nc.semaphore(name))

        ps_s = ctx.enter_context(nc.psum_tensor("ps_s", [P, 2, BANK], F32))
        ps_t = ctx.enter_context(nc.psum_tensor("ps_t", [P, 3, BANK], F32))
        ps_g = ctx.enter_context(nc.psum_tensor("ps_g", [P, BANK], F32))
        ps_y = ctx.enter_context(nc.psum_tensor("ps_y", [P, BANK], F32))
        ps_z = ctx.enter_context(nc.psum_tensor("ps_z", [P, BANK], F32))

        ident = sb("ident", [P, P], F32)
        mask = sb("mask", [P, T], F32)
        iota8 = sb("iota8", [P, QT, E], F32)
        eps_in = sb("eps_in", [P, 2, QT], F32)
        wg = sb("wg", [P, E], F32)
        vt = sb("vt", [P, 2, H * DV], F32R)
        wc = sb("wc", [P, 2, HP * D], F32R)
        w1 = sb("w1", [P, 2, E * F], F32R)
        w2 = sb("w2", [P, 2, FT * D], F32R)
        w_raw = sb("w_raw", [P, 2, E * F], F32)
        w_raw1, w_raw2 = w_raw[:, 0, :], w_raw[:, 1, :]
        zeros = sb("zeros", [P, BANK], F32)
        zeros_b = zeros[:, :].bitcast(BF16)
        v1 = sb("v1", [P, 2, QT, H, VW], BF16)
        v2 = sb("v2", [P, 2, QT, H, DV], BF16)
        v3 = sb("v3", [P, 2, QT, H, DV], BF16)
        v_rest = sb("v_rest", [P, 2, BANK], F32)
        g_hi = sb("g_hi", [P, 2, T], F32R)
        g_lo = sb("g_lo", [P, 2, T], F32R)
        p = sb("p", [P, 2, NBLK * P], F32)
        neg_max = sb("neg_max", [P, 2, QT], F32)
        x1 = sb("x1", [P, B, QT, D], F32)
        sel_raw = sb("sel_raw", [2 * E, E * P], F32)
        a_st = sb("a_st", [P, 2, 2 * P], F32R)
        xt = sb("xt", [P, 2, 2, T], F32R)

        xt_in = sem("xt_in")
        xv_in = sem("xv_in")
        x_in = sem("x_in")
        wz_in = sem("wz_in")
        x1_in = sem("x1_in")
        out_stored = sem("out_stored")
        wait_carrier = sem("wait_carrier")
        g_filled, g_hi_done, g_lo_done = sem("g_filled"), sem("g_hi_done"), sem("g_lo_done")
        s_filled, max_done, exp_done = sem("s_filled"), sem("max_done"), sem("exp_done")
        pt_filled, pt_hi_done, pt_lo_done = sem("pt_filled"), sem("pt_hi_done"), sem("pt_lo_done")
        pv_filled, recip_done, y_done = sem("pv_filled"), sem("recip_done"), sem("y_done")
        v_filled, v1_done, v_full_done = sem("v_filled"), sem("v1_done"), sem("v_full_done")
        v_rest_done, v2_done, v3_done = sem("v_rest_done"), sem("v2_done"), sem("v3_done")
        first_v1, first_rest, first_v2, first_dve, first_pool = (
            sem("first_v1"), sem("first_rest"), sem("first_v2"), sem("first_dve"), sem("first_pool"))
        yt_filled, yt_hi_done, yt_lo_done = sem("yt_filled"), sem("yt_hi_done"), sem("yt_lo_done")
        z_step, zt_done, zn_filled, zn_taken = sem("z_step"), sem("zt_done"), sem("zn_filled"), sem("zn_taken")
        ln1_step, ln1_rstd = sem("ln1_step"), sem("ln1_rstd")
        x1t_filled, x1t_done, x1t_hi_done, x1t_lo_done = (sem("x1t_filled"), sem("x1t_done"), sem("x1t_hi_done"),
                                                          sem("x1t_lo_done"))
        logit_filled, gate_step, gate_exp = sem("logit_filled"), sem("gate_step"), sem("gate_exp")
        ct_filled, ct_done = sem("ct_filled"), sem("ct_done")
        sel_step = sem("sel_step")
        c_filled, c_done = sem("c_filled"), sem("c_done")
        up_filled, hid_done, hid_hi_done, hid_lo_done = (sem("up_filled"), sem("hid_done"), sem("hid_hi_done"),
                                                         sem("hid_lo_done"))
        down_step, col2_done, on_filled = sem("down_step"), sem("col2_done"), sem("on_filled")
        ln2_step, ln2_rstd, on_taken = sem("ln2_step"), sem("ln2_rstd"), sem("on_taken")

        def three_passes(dst, w_parts, m_parts, start=True, stop=True):
            for k, (a, b) in enumerate(((0, 0), (0, 1), (1, 0))):
                last = nc.tensor.matmul(dst, w_parts[a], m_parts[b], start=start and k == 0, stop=stop and k == 2)
            return last

        def wait_apart(eng, semaphore, value):
            eng.wait_ge(semaphore, value)
            eng.sem_inc(wait_carrier, 1)

        def row_max(dve, n, k, q, guard=None):
            if q == 0 and guard is not None:
                wait_apart(dve, pt_filled, guard)
            if q != 1:
                wait_apart(dve, s_filled, PIECES * n + S_PIECE[q] + 1)
            w = (q + 1) * P
            nc.vector.tensor_tensor_reduce(
                p[:, k, blk(q, 0) * P:(blk(q, q) + 1) * P],
                ps_s[:, (k + S_PIECE[q]) % 2, S_AT[q]:S_AT[q] + w], mask[:, T - w:T], -1.0, 3e38, ALU.add,
                ALU.min, neg_max[:, k, q:q + 1]).then_inc(max_done, 1)

        def scores(pe, n, k, slot, piece, guard):
            if guard is not None:
                pe.wait_ge(max_done, guard)
            for q in range(QT):
                if S_PIECE[q] == piece:
                    ins = three_passes(ps_s[:, (k + piece) % 2, S_AT[q]:S_AT[q] + S_COLS[q]],
                                       [g[:, k, q * P:(q + 1) * P] for g in (g_hi, g_lo)],
                                       [xt[:, slot, c, 0:S_COLS[q]] for c in range(2)])
            ins.then_inc(s_filled, 1)

        a_all = w_raw[:, :, :].bitcast(F32R).rearrange("p q (h k c) -> p (q h) k c", k=2, c=P)
        xt_rest = x1[:, :, :, :].bitcast(F32R).rearrange("p (b k) t d -> p b k (t d)", k=2)

        in_q, in_k, in_v, in_w, in_w12, in_wg = [
            sem(f"loaded_{n}") for n in ("q", "k", "v", "w", "w12", "wg")]
        in_x = [sem(f"loaded_x{b}") for b in range(B)]
        const_step = sem("const_step")
        setup_filled = sem("setup_filled")
        setup_hi = sem("setup_hi")
        setup_lo = sem("setup_lo")
        w_hi = sem("w_hi")
        w_lo = sem("w_lo")
        w_sorted = sem("w_sorted")
        xt_out = sem("xt_out")
        a_out = sem("a_out")
        a_in = [sem(f"a_in_{k}") for k in range(2)]

        with ExitStack() as sctx:
            x_raw = sb("x_raw", [P, B * QT, D], F32, sctx)
            q_raw = sb("q_raw", [DQ, D * H], F32, sctx)
            k_raw = sb("k_raw", [DQ, D * H], F32, sctx)
            v_raw = sb("v_raw", [DV, D * H], F32, sctx)
            wo_raw = sb("wo_raw", [D, DV * H], F32, sctx)
            w_h = sb("w_h", [D, H * DV], F32, sctx)

            q_h = q_raw[:, :].rearrange("q (d h) -> q h d", h=H)
            k_h = k_raw[:, :].rearrange("q (d h) -> q h d", h=H)
            v_h = v_raw[:, :].rearrange("v (d h) -> v h d", h=H)

            def setup_bank(k):
                return [ps_t[:, 0, :], ps_t[:, 1, :], ps_t[:, 2, :], ps_g[:, :], ps_y[:, :],
                        ps_z[:, :]][k % BANKS]

            BANKS = 6
            jobs = [("x", 0), ("a", 0), ("v", 0), ("v", 1), ("u", 0), ("u", 1), ("g", 0), ("u", 2), ("u", 3),
                    ("s", 0), ("a", 1), ("u", 4), ("s", 1), ("u", 5), ("a", 2), ("u", 6), ("u", 7), ("g", 1),
                    ("a", 3), ("x", 1), ("x", 2), ("x", 3), ("w", 0), ("w", 1)]
            filling = [j for j in jobs if j[0] != "s"]
            splits = [j for j in filling if j[0] != "u"]

            def taken(pe, j):
                kind, n = filling[j]
                if kind != "u":
                    pe.wait_ge(setup_lo, done_by(kind, n))
                else:
                    pe.wait_ge(first_rest, n + 1)

            def done_by(kind, n):
                return splits.index((kind, n)) + 1

            def job_out(kind, n, part):
                if kind == "x":
                    return (xt[:, n, part, :] if n < 2 else xt_rest[:, n - 2, part, :]), 1.0
                if kind == "a":
                    return a_all[:, 4 * n:4 * n + 4, part, :], QK_SCALE
                if kind == "g":
                    return (g_hi, g_lo)[part][:, n, :], 1.0
                if kind == "v":
                    return vt[:, part, n * BANK:(n + 1) * BANK], 1.0
                return wc[:, part, n * BANK:(n + 1) * BANK], Z_SCALE

            def job_in(k, kind):
                bank = setup_bank(k)
                return bank.rearrange("p (h d) -> p h d", h=4) if kind == "a" else bank

            def odd_unit_before(k):
                kind, n = filling[k - 2] if k >= 2 else ("", 0)
                return n if kind == "u" and n % 2 == 1 else None

            def first_unit(u):
                return (v_rest[:, u % 2, :].rearrange("p (h v) -> p h v", v=DV),
                        (slice(None), 0, u // 2, slice(u % 2 * 8, u % 2 * 8 + 8)))

            with nc.Block() as block:
                @block.sync
                def _(sp):
                    sp.dma_start(x_raw[:, 0:QT, :], x_tiles[0]).then_inc(in_x[0], 16)
                    sp.dma_start(k_raw[:, :], K.rearrange("q d h -> q (d h)")).then_inc(in_k, 16)
                    for b in range(1, B):
                        sp.dma_start(x_raw[:, b * QT:(b + 1) * QT, :], x_tiles[b]).then_inc(in_x[b], 16)
                    sp.wait_ge(setup_lo, done_by("a", 0))
                    for k in range(2):
                        sp.dma_start(a_st[:, k, :].bitcast(F32),
                                     a_all[:, k].bitcast(F32).rearrange("p k c -> p (k c)")).then_inc(a_in[k], 16)
                    for n in range(H // 4):
                        sp.wait_ge(setup_lo, done_by("a", n))
                        sp.dma_start(a_dram[4 * n:4 * n + 4].rearrange("h p c -> p h c"),
                                     a_all[:, 4 * n:4 * n + 4].bitcast(F32).rearrange("p h k c -> p h (k c)")
                                     ).then_inc(a_out, 16)

                @block.gpsimd
                def _(pool):
                    pool.memset(ident[:, :], 0.0).then_inc(const_step, 1)
                    pool.wait_ge(const_step, 1)
                    pool.affine_select(out=ident[:, :], in_=ident[:, :], compare_op=ALU.not_equal, fill=1.0, base=0,
                                       pattern=[[-1, P]], channel_multiplier=1).then_inc(const_step, 1)
                    pool.memset(mask[:, :], 0.0).then_inc(const_step, 1)
                    pool.memset(eps_in[:, 1, :], -0.5).then_inc(const_step, 1)
                    pool.iota(iota8[:, :, :], pattern=[[0, QT], [1, E]], base=0, channel_multiplier=0,
                              allow_small_or_imprecise_dtypes=True).then_inc(const_step, 1)
                    pool.wait_ge(const_step, 3)
                    pool.affine_select(out=mask[:, T - P:T], in_=mask[:, T - P:T], compare_op=ALU.is_ge, fill=MASKED,
                                       base=0, pattern=[[-1, P]], channel_multiplier=1).then_inc(const_step, 1)
                    pool.memset(zeros[:, :], 0.0).then_inc(const_step, 1)
                    pool.memset(v1[:, :, :, :, DV:VW], 1.0).then_inc(const_step, 1)
                    pool.wait_ge(const_step, 8)
                    pool.wait_ge(in_w, 16)
                    for i in range(2):
                        hs = slice(i * 8, i * 8 + 8)
                        pool.tensor_tensor(w_h[:, :].rearrange("d (h v) -> d h v", h=H)[:, hs],
                                           wo_raw[:, :].rearrange("d (v h) -> d h v", h=H)[:, hs],
                                           zeros[:, :].rearrange("p (h v) -> p h v", v=DV),
                                           ALU.add).then_inc(w_sorted, 1)
                    for s, u in enumerate(range(0, UNITS, 2)):
                        rest, at = first_unit(u)
                        pool.wait_ge(first_rest, u + 1)
                        pool.tensor_tensor(v2[at], rest, zeros[:, :].rearrange("p (h v) -> p h v", v=DV),
                                           ALU.add).then_inc(first_pool, 1)
                        pool.wait_ge(first_pool, 2 * s + 1)
                        pool.tensor_tensor(v3[at], rest, v2[at], ALU.subtract).then_inc(first_pool, 1)

                @block.scalar
                def _(act):
                    act.dma_start(q_raw[:, :], Q.rearrange("q d h -> q (d h)")).then_inc(in_q, 16)
                    act.dma_start(v_raw[:, :], V.rearrange("v d h -> v (d h)")).then_inc(in_v, 16)
                    act.dma_start(wo_raw[:, :], W.rearrange("d v h -> d (v h)")).then_inc(in_w, 16)
                    act.dma_start(wg[:, :], Wg).then_inc(in_wg, 16)
                    act.wait_ge(const_step, 8)
                    for k, (kind, n) in enumerate(filling):
                        act.wait_ge(setup_filled, k + 1)
                        if kind == "u":
                            at = first_unit(n)[1]
                            nc.scalar.activation(v1[(*at, slice(0, DV))],
                                                 setup_bank(k).rearrange("p (h v) -> p h v", v=DV),
                                                 ACT.Copy).then_inc(first_v1, 1)
                        else:
                            dst, scale = job_out(kind, n, 0)
                            nc.scalar.activation(dst, job_in(k, kind), ACT.Copy, scale=scale).then_inc(setup_hi, 1)
                        odd = odd_unit_before(k)
                        if odd is not None:
                            rest, at = first_unit(odd)
                            act.wait_ge(first_rest, odd + 1)
                            nc.scalar.activation(v2[at], rest, ACT.Copy).then_inc(first_v2, 1)

                @block.vector
                def _(dve):
                    k = 0
                    for kind, n in jobs:
                        if kind == "s":
                            dve.wait_ge(const_step, 6)
                            for q in ((0, 1, 2) if n == 0 else (3,)):
                                row_max(dve, 0, 0, q)
                            continue
                        if kind == "u":
                            rest, at = first_unit(n)
                            if n >= 2 and n % 2 == 0:
                                dve.wait_ge(first_pool, n)
                            dve.wait_ge(first_v1, n + 1)
                            nc.vector.tensor_tensor(rest, setup_bank(k).rearrange("p (h v) -> p h v", v=DV),
                                                    v1[(*at, slice(0, DV))], ALU.subtract).then_inc(first_rest, 1)
                        else:
                            dve.wait_ge(setup_hi, done_by(kind, n))
                            dst, scale = job_out(kind, n, 1)
                            nc.vector.scalar_tensor_tensor(out=dst, in0=job_in(k, kind), scalar=scale,
                                                           in1=job_out(kind, n, 0)[0], op0=ALU.mult,
                                                           op1=ALU.subtract).then_inc(setup_lo, 1)
                        odd = odd_unit_before(k)
                        if odd is not None:
                            rest, at = first_unit(odd)
                            dve.wait_ge(first_v2, odd // 2 + 1)
                            nc.vector.tensor_tensor(v3[at], rest, v2[at], ALU.subtract).then_inc(first_dve, 1)
                            dve.wait_ge(first_dve, odd // 2 + 1)
                        k += 1

                @block.tensor
                def _(pe):
                    pe.wait_ge(const_step, 2)
                    k = 0
                    for kind, n in jobs:
                        if kind == "s":
                            pe.wait_ge(setup_lo, done_by("g", 0))
                            for piece in ((0, 1) if n == 0 else (2,)):
                                scores(pe, 0, 0, 0, piece, 2 if piece == 2 else None)
                            continue
                        if k >= BANKS:
                            taken(pe, k - BANKS)
                        bank = setup_bank(k)
                        k += 1
                        if kind == "u":
                            if n < 2:
                                pe.wait_ge(setup_lo, done_by("v", n))
                            t = n // 2
                            last = three_passes(bank, [xt[:, 0, q, t * P:(t + 1) * P] for q in range(2)],
                                                [vt[:, q, n % 2 * BANK:(n % 2 + 1) * BANK] for q in range(2)])
                        elif kind == "g":
                            pe.wait_ge(a_in[n], 16)
                            pe.wait_ge(setup_lo, done_by("x", 0))
                            last = three_passes(bank, [a_st[:, n, q * P:(q + 1) * P] for q in range(2)],
                                                [xt[:, 0, q, :] for q in range(2)])
                        elif kind == "x":
                            pe.wait_ge(in_x[n], 16)
                            for t in range(QT):
                                last = nc.tensor.transpose(bank[:, t * P:(t + 1) * P], x_raw[:, n * QT + t, :],
                                                           ident[:, :])
                        elif kind == "a":
                            if n == 0:
                                pe.wait_ge(in_q, 16)
                                pe.wait_ge(in_k, 16)
                            for h in range(4):
                                last = nc.tensor.matmul(bank[:, h * P:(h + 1) * P], q_h[:, 4 * n + h, :],
                                                        k_h[:, 4 * n + h, :], start=True, stop=True)
                        elif kind == "v":
                            if n == 0:
                                pe.wait_ge(in_v, 16)
                            for h in range(8):
                                last = nc.tensor.transpose(bank[:, h * DV:(h + 1) * DV], v_h[:, 8 * n + h, :],
                                                           ident[0:DV, 0:DV])
                        else:
                            pe.wait_ge(w_sorted, 2)
                            for c in range(4):
                                last = nc.tensor.transpose(bank[:, c * P:(c + 1) * P],
                                                           w_h[:, (4 * n + c) * P:(4 * n + c + 1) * P], ident[:, :])
                        last.then_inc(setup_filled, 1)

        xv = sb("xv", [P, 2, P], F32R)
        x_nat = sb("x_nat", [P, QT, D], F32)
        sel = sb("sel", [2 * E, E * P], F32R)
        ct = sb("ct", [2 * E, T], F32R)
        comb_parts = sb("comb_parts", [P, QT, 2 * E], F32R)
        v_full = sb("v_full", [P, BANK], F32)
        wz = sb("wz", [P, 2, P], F32R)
        pt_hi = sb("pt_hi", [P, 2, NBLK * P], F16)
        pt_lo = sb("pt_lo", [P, 2, NBLK * P], F16)
        y = sb("y", [P, QT, 2 * DV], F32)
        r_sum = sb("r_sum", [P, QT], F32)
        yt_hi = sb("yt_hi", [P, T], F32R)
        yt_lo = sb("yt_lo", [P, T], F32R)
        col = sb("col", [P, T], F32)
        res = sb("res", [P, QT, D], F32)
        st = sb("st", [P, QT, 6], F32)
        mv = sb("mv", [P, QT, 2], F32)
        rstd = sb("rstd", [P, QT], F32)
        logit = sb("logit", [P, QT, E], F32)
        best = sb("best", [P, QT, E], F32)
        best_at = sb("best_at", [P, QT, E], U32)
        at_f = sb("at_f", [P, QT, TOP], F32)
        gate = sb("gate", [P, 5, QT], F32)
        pick = sb("pick", [P, 2, QT, E], F32)
        comb = sb("comb", [P, QT, E], F32)
        p_flat = p[:, :, :].rearrange("p k c -> p (k c)")
        hid = [p_flat[:, i * BANK:(i + 1) * BANK] for i in range(RING)]
        c_row = [p_flat[:, RING * BANK:(RING + 1) * BANK], v_rest[:, 1, :]]
        hid_hi = [g_hi[:, 0, :], g_hi[:, 1, :], yt_hi[:, :], vt[:, 0, 0:BANK]]
        hid_lo = [g_lo[:, 0, :], g_lo[:, 1, :], yt_lo[:, :], vt[:, 1, 0:BANK]]
        up_bank = [ps_t[:, 0, :], ps_t[:, 1, :], ps_t[:, 2, :], ps_s[:, 1, :]]
        row_bank = ps_s[:, 0, :]

        def logit_bank(b):
            return ps_g[:, :] if isinstance(b, int) else ps_y[:, :]

        def rows_bank(b):
            return ps_s[:, 1, :] if isinstance(b, int) else ps_y[:, :]

        x1t = v_full
        x1_fix = v_rest[:, 0, :]
        x1t_parts = xt
        x2 = x_nat

        LN_STEPS = 1 + QT + QT + 1 + QT
        Z_STEPS = HP + 1
        V_BASE = 1
        GATE_SPLIT = 1 + QT + QT + 1 + 1 + TOP
        GATE_STEPS = 1 + QT + QT + 1 + 1 + TOP + 3 + TOP + 3

        def attention(eng, start, pair, first_pair, second_pair, end):
            def middle(b, final):
                with eng.Fori(2, HP - 2, 2) as i:
                    pair(b, i, False, final)
                    pair(b, i + 1, False, final)
                pair(b, HP - 2, False, final)
                pair(b, HP - 1, True, final)

            start()
            with eng.Fori(0, B - 1) as b:
                middle(b, False)
                first_pair(b)
                second_pair(b)
            middle(B - 1, True)
            end()


        def experts(eng, stage):
            for s in range(ROTATE):
                stage(0, s, False)
            with eng.Fori(0, B - 1) as b:
                for s in range(ROTATE, FT + ROTATE):
                    stage(b, s, False)
            for s in range(ROTATE, FT + OUT_AT):
                stage(B - 1, s, True)

        with nc.Block() as block:
            @block.sync
            def _(sp):
                sp.sem_inc(out_stored, 16)

                def load_a(n, k, head):
                    sp.wait_ge(g_filled, n + 1)
                    sp.dma_start(a_st[:, k, :].bitcast(F32), a_dram[head]).then_inc(a_in[k], 16)

                def load_first_a(n, k, head):
                    sp.wait_ge(g_filled, n + 1)
                    sp.dma_start(a_st[:, k, :].bitcast(F32),
                                 a_all[:, head].bitcast(F32).rearrange("p k c -> p (k c)")).then_inc(a_in[k], 16)

                def load_wz(b, c):
                    sp.wait_ge(z_step, Z_STEPS * b + c + 1)
                    sp.dma_start(wz[:, :, :].bitcast(F32),
                                 wc[:, :, bass.ds(c * P, P)].bitcast(F32)).then_inc(wz_in, 16)

                def load_xv(b, j):
                    sp.wait_ge(v_filled, b * UNITS + j + UNITS)
                    sp.dma_start(xv[:, :, :].bitcast(F32),
                                 xt[:, (b + 1) % 2, :, bass.ds(j % QT * P, P)].bitcast(F32)).then_inc(xv_in, 16)

                def start():
                    sp.sem_inc(in_w12, 16)
                    sp.sem_inc(xt_in, 16)
                    for n in range(4):
                        load_first_a(n, n % 2, n + 2)
                        if n == 1:
                            sp.dma_start(xt_dram[2:B].rearrange("b p k t -> p b k t"),
                                         xt_rest.bitcast(F32)).then_inc(xt_out, 16)
                    sp.wait_ge(a_out, 16 * (H // 4))
                    sp.wait_ge(xt_out, 16)
                    load_wz(0, 0)
                    for k in range(2):
                        load_a(4 + k, k, 6 + k)

                def load_w(e):
                    sp.wait_ge(in_w12, 32 * e + 16)
                    sp.dma_start(w_raw1[:, bass.ds(e * F, F)], W1[e]).then_inc(in_w12, 16)
                    sp.dma_start(w_raw2[:, bass.ds(e * F, F)].rearrange("f (c d) -> f c d", d=D),
                                 w2_tiles[e]).then_inc(in_w12, 16)

                def pair(b, i, last, final):
                    n = b * H + i * 2
                    if not final:
                        wait_apart(sp, xt_in, (b + 1) * 16)
                        load_xv(b, i - 2)
                    if final:
                        load_w(i - 2)
                        if isinstance(i, int) and not last:
                            sp.wait_ge(v3_done, (B - 1) * UNITS + V_BASE)
                            sp.wait_ge(ln1_step, LN_STEPS)
                            stage_x1(0)
                        if last:
                            load_w(i - 1)
                            load_w(i)
                    load_wz(b, i - 1)
                    if last:
                        sp.wait_ge(zn_taken, b + 1)
                        sp.dma_start(x_nat[:, :, :], x_tiles[b]).then_inc(x_in, 16)
                    if not (final and last):
                        for k in range(2):
                            load_a(n + k + 2, k, (2 * i + k + 4) % H)

                def first_pair(b):
                    n = (b + 1) * H
                    sp.wait_ge(s_filled, PIECES * n)
                    sp.dma_start(xt[:, b % 2, :, :].bitcast(F32), xt_dram[b % 2 + 2]).then_inc(xt_in, 16)
                    load_xv(b, UNITS - 2)
                    load_wz(b, HP - 1)
                    for k in range(2):
                        load_a(n + k + 2, k, k + 4)

                def second_pair(b):
                    n = (b + 1) * H + 2
                    load_xv(b, UNITS - 1)
                    load_wz(b + 1, 0)
                    for k in range(2):
                        load_a(n + k + 2, k, k + 6)

                def stage_x1(b):
                    sp.dma_start(x1_fix, x1[:, b, :, :].rearrange("p t d -> p (t d)")).then_inc(x1_in, 16)

                def end():
                    load_wz(B - 1, HP - 1)
                    sp.wait_ge(x1t_filled, 1)
                    sp.wait_ge(ln1_step, 2 * LN_STEPS)
                    stage_x1(1)

                attention(sp, start, pair, first_pair, second_pair, end)

                def stage(b, s, final):
                    if s == PREP_X1T and not final:
                        sp.wait_ge(ln1_step, LN_STEPS * B)
                        sp.wait_ge(x1t_filled, b + 2)
                        stage_x1((b + 2) % B)
                    if s == FT + OUT_AT - final:
                        for lo, hi in ((0, QT // 2), (QT // 2, QT)) if final else ((0, QT),):
                            sp.wait_ge(ln2_step, LN_STEPS * (b + 1) + 1 - (QT - hi))
                            sp.dma_start(out_tiles[b][:, lo:hi], x2[:, lo:hi, :]).then_inc(out_stored, 16)

                experts(sp, stage)
                sp.wait_ge(out_stored, 16 * (B + 2))
                sp.wait_ge(x1_in, 16 * (B + 1))
                sp.wait_ge(xt_in, 16 * B)
                for k in range(2):
                    sp.wait_ge(a_in[k], 16 * (B * HP + 1))

            @block.gpsimd
            def _(pool):
                pool.memset(sel_raw[:, :], 0.0).then_inc(sel_step, 1)
                for r in range(2):
                    pool.wait_ge(sel_step, r + 1)
                    pool.affine_select(out=sel_raw[:, :].rearrange("p (e c) -> p e c", e=E),
                                       in_=sel_raw[:, :].rearrange("p (e c) -> p e c", e=E),
                                       compare_op=ALU.not_equal, fill=1.0, base=-r * E,
                                       pattern=[[-1, E], [0, P]], channel_multiplier=1).then_inc(sel_step, 1)

                pool.sem_inc(v_rest_done, V_BASE)
                pool.sem_inc(v2_done, V_BASE)
                pool.sem_inc(v3_done, V_BASE)

                def split_v(s, slot, t, half):
                    hs = bass.ds(half * 8, 8)
                    rest = v_rest[:, 0, :].rearrange("p (h v) -> p h v", v=DV)
                    pool.wait_ge(v3_done, s)
                    pool.wait_ge(v_full_done, s + 1)
                    pool.tensor_tensor(rest, v_full[:, :].rearrange("p (h v) -> p h v", v=DV),
                                       v1[:, slot, t, hs, 0:DV], ALU.subtract).then_inc(v_rest_done, 1)
                    pool.wait_ge(v_rest_done, s + 1)
                    pool.tensor_tensor(v2[:, slot, t, hs, :], rest,
                                       zeros[:, :].rearrange("p (h v) -> p h v", v=DV), ALU.add).then_inc(v2_done, 1)
                    pool.wait_ge(v2_done, s + 1)
                    pool.tensor_tensor(v3[:, slot, t, hs, :], rest, v2[:, slot, t, hs, :],
                                       ALU.subtract).then_inc(v3_done, 1)

                def split_w(c):
                    at = bass.ds(c * F, F)
                    for q, (w, raw) in enumerate(((w1, w_raw1), (w2, w_raw2))):
                        pool.wait_ge(w_hi, 2 * c + q + 1)
                        pool.tensor_tensor(w[:, 1, at], raw[:, at], w[:, 0, at], ALU.subtract).then_inc(w_lo, 1)

                def pair(b, i, last, final):
                    if not final:
                        split_v(b * UNITS + i - 2 + V_BASE, (b + 1) % 2, (i - 2) % QT, (i - 2) // QT)
                    else:
                        split_w(i - 2)
                        if last:
                            split_w(i - 1)
                            split_w(i)

                def rstd_of(step_sem, rstd_sem, b):
                    pool.wait_ge(step_sem, LN_STEPS * b + 2 + 2 * QT + (1 if step_sem is ln2_step else 0))
                    pool.tensor_tensor(rstd[:, :], eps_in[:, 0, :], eps_in[:, 1, :], ALU.pow).then_inc(rstd_sem, 1)

                def first_pair(b):
                    split_v(b * UNITS + UNITS - 2 + V_BASE, (b + 1) % 2, QT - 2, 1)

                def second_pair(b):
                    rstd_of(ln1_step, ln1_rstd, b)
                    split_v(b * UNITS + UNITS - 1 + V_BASE, (b + 1) % 2, QT - 1, 1)

                attention(pool, lambda: None, pair, first_pair, second_pair, lambda: None)

                def stage(b, s, final):
                    if s < FT or not final:
                        pool.wait_ge(hid_hi_done, FT * b + s + 1)
                        if not isinstance(b, int) or b > 0 or s >= RING:
                            pool.wait_ge(down_step, FT * b + s - RING + 1)
                        pool.tensor_tensor(hid_lo[s % RING], hid[s % RING], hid_hi[s % RING],
                                           ALU.subtract).then_inc(hid_lo_done, 1)
                    if s == 3:
                        rstd_of(ln1_step, ln1_rstd, B - 1)
                    if s == FT + OUT_AT - final:
                        rstd_of(ln2_step, ln2_rstd, b)

                experts(pool, stage)

            @block.scalar
            def _(act):
                def v_high(m, s, slot, t, half, bank):
                    hs = bass.ds(half * 8, 8)
                    act.wait_ge(v_filled, m + 1)
                    nc.scalar.activation(v1[:, slot, t, hs, 0:DV], bank.rearrange("p (h v) -> p h v", v=DV),
                                         ACT.Copy).then_inc(v1_done, 1)
                    act.wait_ge(v1_done, m + 1)
                    act.wait_ge(v3_done, s)
                    nc.scalar.activation(v_full[:, :], bank, ACT.Copy).then_inc(v_full_done, 1)

                def g_high(n, k):
                    act.wait_ge(g_filled, n + 1)
                    nc.scalar.activation(g_hi[:, k, :], ps_g[:, :], ACT.Copy).then_inc(g_hi_done, 1)

                def yt_high(b, c, bank):
                    act.wait_ge(yt_filled, b * HP + c + 1)
                    act.wait_ge(z_step, Z_STEPS * b + c + 1)
                    nc.scalar.activation(yt_hi[:, :], bank, ACT.Copy).then_inc(yt_hi_done, 1)

                def start():
                    act.sem_inc(g_hi_done, 2)
                    act.sem_inc(v1_done, UNITS)
                    act.sem_inc(v_full_done, V_BASE)
                    for k in range(2):
                        step(k, k, k)
                    second(0)
                    act.wait_ge(sel_step, 3)
                    nc.scalar.activation(sel[:, :], sel_raw[:, :], ACT.Copy).then_inc(sel_step, 1)

                def split_w(c):
                    at = bass.ds(c * F, F)
                    act.wait_ge(in_w12, 32 * c + 48)
                    for w, raw in ((w1, w_raw1), (w2, w_raw2)):
                        nc.scalar.activation(w[:, 0, at], raw[:, at], ACT.Copy).then_inc(w_hi, 1)

                def pt_high(n, k, c):
                    lo, hi = PT_PIECES[c]
                    act.wait_ge(pt_filled, 2 * n + c + 1)
                    nc.scalar.activation(pt_hi[:, k, lo * P:hi * P],
                                         ps_t[:, :, :].rearrange("p k c -> p (k c)")[:, lo * P:hi * P],
                                         ACT.Copy, scale=P_SCALE).then_inc(pt_hi_done, 1)

                def step(n, k, static_n=None, unit=None, split=(), chunk=None, z_of=None, ahead=True,
                         last_pair=False, second_last=False):
                    for q in range(QT):
                        act.wait_ge(max_done, n * QT + q + 1)
                        at = slice(blk(q, 0) * P, (blk(q, q) + 1) * P)
                        nc.scalar.activation(p[:, k, at], p[:, k, at], ACT.Exp, bias=neg_max[:, k, q:q + 1],
                                             scale=-1.0).then_inc(exp_done, 1)
                    if last_pair and k == 1:
                        gate_part(0)
                    if z_of is not None:
                        act.wait_ge(z_step, Z_STEPS * (z_of + 1))
                        nc.scalar.activation(col[:, :], ps_z[:, :], ACT.Copy).then_inc(zt_done, 1)
                    if ahead:
                        act.wait_ge(s_filled, PIECES * (n + 1))
                        g_high(n + 2, k)
                    if static_n is None:
                        act.wait_ge(pv_filled, n - 1)
                    pt_high(n, k, 0)
                    if chunk is not None:
                        yt_high(*chunk, ps_g[:, :])
                    pt_high(n, k, 1)
                    if unit is not None:
                        b, j = unit
                        v_high(b * UNITS + j + UNITS, b * UNITS + j + V_BASE, (b + 1) % 2, j % QT, j // QT,
                               ps_g[:, :])
                    if second_last and k == 0:
                        act.wait_ge(v3_done, (B - 1) * UNITS + V_BASE)
                        take_x1t(0)
                    for e in split:
                        split_w(e)

                def pair(b, i, last, final):
                    n = b * H + 2 * i
                    ahead = not (last and final)
                    step(n, 0, unit=None if final else (b, i - 2), split=(i - 2,) if final else (), ahead=ahead,
                         second_last=final and isinstance(i, int) and not last)
                    step(n + 1, 1, chunk=(b, i - 1), split=(i - 1, i) if final and last else (), ahead=ahead,
                         last_pair=not ahead)

                def first_pair(b):
                    n = (b + 1) * H
                    step(n, 0, unit=(b, UNITS - 2))
                    step(n + 1, 1, chunk=(b, HP - 1))

                def second(b, unit=None, z_of=None):
                    step(b * H + 2, 0, unit=unit, z_of=z_of)
                    step(b * H + 3, 1, chunk=(b, 0))

                def second_pair(b):
                    second(b + 1, (b, UNITS - 1), b)

                def take_x1t(b):
                    act.wait_ge(x1t_filled, b + 1)
                    nc.scalar.activation(x1t[:, :], ps_g[:, :], ACT.Copy).then_inc(x1t_done, 1)

                def gate_part(b):
                    act.wait_ge(gate_step, GATE_STEPS * b + 2 + 2 * QT)
                    nc.scalar.activation(gate[:, 1, :], gate[:, 0, :], ACT.Exp).then_inc(gate_exp, 1)

                def take_ct(b):
                    act.wait_ge(ct_filled, b + 1)
                    nc.scalar.activation(ct[:, :], rows_bank(b)[0:2 * E], ACT.Copy).then_inc(ct_done, 1)

                def end():
                    take_ct(0)
                    yt_high(B - 1, HP - 1, ps_g[:, :])

                attention(act, start, pair, first_pair, second_pair, end)

                def take_row(b, e):
                    act.wait_ge(c_filled, E * b + e + 1)
                    if not isinstance(b, int) or b > 0 or e >= 2:
                        act.wait_ge(hid_done, FT * b + (e - 1) * FPE)
                    nc.scalar.activation(c_row[e % 2], row_bank, ACT.Copy).then_inc(c_done, 1)

                def stage(b, s, final):
                    if s < FT or not final:
                        if s == 0:
                            take_row(b, 0)
                        if s % FPE == 1 and (s + 1 < FT or not final):
                            take_row(b, (s + 1) // FPE)
                        act.wait_ge(hid_done, FT * b + s + 1)
                        if not isinstance(b, int) or b > 0 or s >= RING:
                            act.wait_ge(down_step, FT * b + s - RING + 1)
                        nc.scalar.activation(hid_hi[s % RING], hid[s % RING], ACT.Copy).then_inc(hid_hi_done, 1)
                    if s == 0:
                        act.wait_ge(z_step, Z_STEPS * B)
                        nc.scalar.activation(col[:, :], ps_z[:, :], ACT.Copy).then_inc(zt_done, 1)
                    if not final and s == PREP_X1T:
                        take_x1t(b + 1)
                    if not final and s == PREP_GATE:
                        gate_part(b + 1)
                    if not final and s == PREP_ROWS:
                        take_ct(b + 1)
                    if s == FT + OUT_AT - 1:
                        act.wait_ge(down_step, FT * (b + 1))
                        nc.scalar.activation(col[:, :], ps_z[:, :], ACT.Copy).then_inc(col2_done, 1)

                experts(act, stage)

            @block.vector
            def _(dve):
                def g_low(n, k):
                    dve.wait_ge(g_hi_done, n + 1)
                    nc.vector.tensor_tensor(g_lo[:, k, :], ps_g[:, :], g_hi[:, k, :],
                                            ALU.subtract).then_inc(g_lo_done, 1)

                def norm(n, k):
                    ps = ps_y[:, 0:QT * VW].rearrange("p (t c) -> p t c", c=VW)
                    dve.wait_ge(pv_filled, n + 1)
                    nc.vector.reciprocal(r_sum[:, :], ps[:, :, DV]).then_inc(recip_done, 1)
                    dve.wait_ge(recip_done, n + 1)
                    nc.vector.tensor_tensor(y[:, :, k * DV:(k + 1) * DV], ps[:, :, 0:DV],
                                            r_sum[:, :].unsqueeze(2).to_broadcast([P, QT, DV]),
                                            ALU.mult).then_inc(y_done, 1)

                def pt_low(n, k, c):
                    lo, hi = PT_PIECES[c]
                    dve.wait_ge(pt_hi_done, 2 * n + c + 1)
                    nc.vector.scalar_tensor_tensor(
                        out=pt_lo[:, k, lo * P:hi * P],
                        in0=ps_t[:, :, :].rearrange("p k c -> p (k c)")[:, lo * P:hi * P], scalar=P_SCALE,
                        in1=pt_hi[:, k, lo * P:hi * P], op0=ALU.mult, op1=ALU.subtract).then_inc(pt_lo_done, 1)

                def yt_low(m, bank):
                    dve.wait_ge(yt_hi_done, m + 1)
                    nc.vector.tensor_tensor(yt_lo[:, :], bank, yt_hi[:, :], ALU.subtract).then_inc(yt_lo_done, 1)

                dve.sem_inc(ln2_step, 1)
                dve.sem_inc(zn_taken, 1)
                dve.sem_inc(on_taken, 1)

                def start():
                    dve.sem_inc(g_lo_done, 2)
                    step(0, 0, free=True, norm_before=False)
                    step(1, 1)
                    step(2, 0)
                    step(3, 1, chunk=0)

                def step(n, k, free=False, chunk=None, z_of=None, more=True, ahead=True, norm_before=True):
                    if more:
                        for q in range(QT - 1):
                            row_max(dve, n + 1, 1 - k, q, None if free else 2 * n)
                    if ahead:
                        g_low(n + 2, k)
                    pt_low(n, k, 0)
                    if more:
                        row_max(dve, n + 1, 1 - k, QT - 1)
                    if chunk is not None:
                        yt_low(chunk, ps_g[:, :])
                    pt_low(n, k, 1)
                    if z_of is not None:
                        first_residual(z_of)
                    if norm_before:
                        norm(n - 1, 1 - k)

                def pair(b, i, last, final):
                    n = b * H + 2 * i
                    ahead = not (last and final)
                    step(n, 0, ahead=ahead)
                    if isinstance(i, int) and not last and isinstance(b, int):
                        dve.wait_ge(xt_in, 16 * B)
                        split_x1t(0)
                    if not ahead:
                        choose(0, 0)
                    step(n + 1, 1, chunk=b * HP + i - 1, more=ahead, ahead=ahead)
                    if not ahead:
                        choose(0, 1)

                def residual(b, step_sem, src, shortcut, filled):
                    dve.wait_ge(filled, b + 1)
                    nc.vector.tensor_tensor(res[:, :, :], src.rearrange("p (t d) -> p t d", d=D), shortcut,
                                            ALU.add).then_inc(step_sem, 1)

                def moments(c, step_sem, taken):
                    wait_apart(dve, step_sem, c + 1)
                    dve.sem_inc(taken, 1)
                    for t in range(QT):
                        nc.vector.bn_stats(st[:, t, :], res[:, t, :]).then_inc(step_sem, 1)
                    wait_apart(dve, step_sem, c + 1 + QT)
                    for t in range(QT):
                        nc.vector.bn_aggr(mv[:, t, :], st[:, t, :]).then_inc(step_sem, 1)
                    dve.wait_ge(step_sem, c + 1 + 2 * QT)
                    nc.vector.tensor_scalar(eps_in[:, 0, :], mv[:, :, 1], EPS, None, ALU.add).then_inc(step_sem, 1)

                def normalise(b, step_sem, rstd_sem, dst, guard):
                    dve.wait_ge(rstd_sem, b + 1)
                    if guard is not None:
                        dve.wait_ge(*guard)
                    for t in range(QT):
                        nc.vector.tensor_scalar(dst[:, t, :], res[:, t, :], mv[:, t, 0:1], rstd[:, t:t + 1],
                                                ALU.subtract, ALU.mult).then_inc(step_sem, 1)

                def first_residual(b):
                    dve.wait_ge(x_in, 16 * (b + 1))
                    residual(b, ln1_step, ps_g[:, :], x_nat[:, :, :], zn_filled)

                def first_norm(b):
                    dve.wait_ge(xt_out, 16)
                    normalise(b, ln1_step, ln1_rstd, x1[:, b, :, :], None)

                def first_pair(b):
                    n = (b + 1) * H
                    step(n, 0)
                    step(n + 1, 1, chunk=b * HP + HP - 1)

                def second_pair(b):
                    n = (b + 1) * H + 2
                    step(n, 0, z_of=b)
                    moments(LN_STEPS * b, ln1_step, zn_taken)
                    step(n + 1, 1, chunk=(b + 1) * HP)
                    first_norm(b)

                def split_x1t(b):
                    slot = b % 2
                    dve.wait_ge(x1t_done, b + 1)
                    nc.vector.tensor_copy(x1t_parts[:, slot, 0, :], x1t[:, :]).then_inc(x1t_hi_done, 1)
                    dve.wait_ge(x1t_hi_done, b + 1)
                    nc.vector.tensor_tensor(x1t_parts[:, slot, 1, :], x1t[:, :], x1t_parts[:, slot, 0, :],
                                            ALU.subtract).then_inc(x1t_lo_done, 1)

                def choose(b, part=None):
                    g = [GATE_STEPS * b + (GATE_SPLIT if part == 1 else 0)]

                    def sync():
                        dve.wait_ge(gate_step, g[0])

                    def did(ins):
                        ins.then_inc(gate_step, 1)
                        g[0] = g[0] + 1

                    if part != 1:
                        largest(b, g, did, sync)
                    if part != 0:
                        weigh(b, g, did, sync)

                def largest(b, g, did, sync):
                    dve.wait_ge(logit_filled, b + 1)
                    did(nc.vector.tensor_copy(logit[:, :, :],
                                              logit_bank(b)[:, 0:QT * E].rearrange("p (t e) -> p t e", e=E)))
                    wait_apart(dve, gate_step, g[0])
                    for t in range(QT):
                        did(nc.vector.max(best[:, t, :], logit[:, t, :]))
                    wait_apart(dve, gate_step, g[0])
                    for t in range(QT):
                        did(nc.vector.max_index(best_at[:, t, :], best[:, t, :], logit[:, t, :]))
                    did(nc.vector.tensor_tensor(gate[:, 0, :], best[:, :, 1], best[:, :, 0], ALU.subtract))
                    sync()
                    did(nc.vector.tensor_copy(at_f[:, :, :], best_at[:, :, 0:TOP]))
                    sync()
                    for k in range(TOP):
                        did(nc.vector.tensor_tensor(pick[:, k, :, :], iota8[:, :, :],
                                                    at_f[:, :, k:k + 1].to_broadcast([P, QT, E]), ALU.is_equal))

                def weigh(b, g, did, sync):
                    dve.wait_ge(gate_exp, b + 1)
                    did(nc.vector.tensor_scalar(gate[:, 2, :], gate[:, 1, :], 1.0, None, ALU.add))
                    sync()
                    did(nc.vector.reciprocal(gate[:, 3, :], gate[:, 2, :]))
                    sync()
                    did(nc.vector.tensor_tensor(gate[:, 4, :], gate[:, 3, :], gate[:, 1, :], ALU.mult))
                    sync()
                    for k in range(TOP):
                        did(nc.vector.tensor_tensor(pick[:, k, :, :], pick[:, k, :, :],
                                                    gate[:, 3 + k, :].unsqueeze(2).to_broadcast([P, QT, E]),
                                                    ALU.mult))
                    sync()
                    did(nc.vector.tensor_tensor(comb[:, :, :], pick[:, 0, :, :], pick[:, 1, :, :], ALU.add))
                    sync()
                    did(nc.vector.tensor_copy(comb_parts[:, :, 0:E], comb[:, :, :]))
                    sync()
                    did(nc.vector.tensor_tensor(comb_parts[:, :, E:2 * E], comb[:, :, :], comb_parts[:, :, 0:E],
                                                ALU.subtract))

                def end():
                    norm(B * H - 1, 1)
                    yt_low(B * HP - 1, ps_g[:, :])

                attention(dve, start, pair, first_pair, second_pair, end)

                def stage(b, s, final):
                    if s < FT or not final:
                        dve.wait_ge(up_filled, FT * b + s + 1)
                        if s % FPE == 0:
                            dve.wait_ge(c_done, E * b + s // FPE + 1)
                        if not isinstance(b, int) or b > 0 or s >= RING:
                            dve.wait_ge(hid_lo_done, FT * b + s - RING + 1)
                        nc.vector.scalar_tensor_tensor(out=hid[s % RING], in0=up_bank[s % RING], scalar=0.0,
                                                       in1=c_row[s // FPE % 2], op0=ALU.max,
                                                       op1=ALU.mult).then_inc(hid_done, 1)
                    if s == 2:
                        first_residual(B - 1)
                        moments(LN_STEPS * (B - 1), ln1_step, zn_taken)
                    if s == 4:
                        first_norm(B - 1)
                    if not final and s == PREP_X1T:
                        split_x1t(b + 1)
                    if not final and s in (PREP_GATE, PREP_GATE + 2):
                        choose(b + 1, (s - PREP_GATE) // 2)
                    if s == FT + OUT_AT - final:
                        residual(b, ln2_step, ps_g[:, :], x1[:, b, :, :], on_filled)
                    if s == (FT + OUT_AT - 1 if final else FT + OUT_AT + 1):
                        moments(LN_STEPS * b + 1, ln2_step, on_taken)
                    if s == FT + OUT_AT + 2 or (final and s == FT + OUT_AT - 1):
                        normalise(b, ln2_step, ln2_rstd, x2[:, :, :], (out_stored, (b + 1) * 16))

                experts(dve, stage)

            @block.tensor
            def _(pe):
                def g_product(n, k, slot):
                    pe.wait_ge(a_in[k], ((n - k) // 2 + 1) * 16)
                    three_passes(ps_g[:, :], [a_st[:, k, q * P:(q + 1) * P] for q in range(2)],
                                 [xt[:, slot, q, :] for q in range(2)]).then_inc(g_filled, 1)

                def p_transpose(n, k, q, first):
                    pe.wait_ge(exp_done, n * QT + q + 1)
                    for j in range(q + 1):
                        m = blk(q, j)
                        if not first and m == 0:
                            pe.wait_ge(pt_lo_done, 2 * n - 1)
                        if not first and m == 4:
                            pe.wait_ge(pt_lo_done, 2 * n)
                        ins = nc.tensor.transpose(ps_t[:, m // 4, (m % 4) * P:(m % 4 + 1) * P],
                                                  p[:, k, m * P:(m + 1) * P], ident[:, :])
                        if m == 3 or m == NBLK - 1:
                            ins.then_inc(pt_filled, 1)

                def pv(n, h, k, slot):
                    pe.wait_ge(pt_lo_done, 2 * n + 2)
                    for q in range(QT):
                        o, o1 = ps_y[:, q * VW:q * VW + DV], ps_y[:, q * VW:(q + 1) * VW]
                        for j in range(q + 1):
                            m = slice(blk(q, j) * P, (blk(q, j) + 1) * P)
                            nc.tensor.matmul(o1, pt_hi[:, k, m], v1[:, slot, j, h, :], start=j == 0, stop=False)
                            nc.tensor.matmul(o, pt_hi[:, k, m], v2[:, slot, j, h, :], start=False, stop=False)
                            nc.tensor.matmul(o, pt_hi[:, k, m], v3[:, slot, j, h, :], start=False, stop=False)
                            ins = nc.tensor.matmul(o1, pt_lo[:, k, m], v1[:, slot, j, h, :], start=False, stop=j == q)
                    ins.then_inc(pv_filled, 1)

                def yt_chunk(m, bank):
                    pe.wait_ge(y_done, 2 * m + 2)
                    for t in range(QT):
                        ins = nc.tensor.transpose(bank[:, t * P:(t + 1) * P], y[:, t, :], ident[:, :])
                    ins.then_inc(yt_filled, 1)

                def open_z():
                    nc.tensor.matmul(ps_z[:, :], zeros_b[:, 0:P], zeros_b[:, 0:T], start=True,
                                     stop=False).then_inc(z_step, 1)

                def z_product(m, last):
                    pe.wait_ge(wz_in, (m + 1) * 16)
                    pe.wait_ge(yt_lo_done, m + 1)
                    three_passes(ps_z[:, :], [wz[:, q, :] for q in range(2)], [yt_hi[:, :], yt_lo[:, :]],
                                 start=False, stop=last).then_inc(z_step, 1)

                def step(n, k, h, slot, next_slot=None, ahead_slot=None, before=True, before_slot=None, v_guard=None,
                         unit=None, chunk=None, z_before=None, z_end=None, free_g=None, static_n=None,
                         extra=None):
                    if next_slot is not None:
                        pe.wait_ge(g_lo_done, n + 2)
                        scores(pe, n + 1, 1 - k, next_slot, 0, n * QT + 3)
                        scores(pe, n + 1, 1 - k, next_slot, 1, n * QT + 4)
                    if z_before is not None:
                        z_product(z_before, z_end is not None)
                    if ahead_slot is not None:
                        if free_g is not None:
                            pe.wait_ge(v_full_done, free_g)
                        g_product(n + 2, k, ahead_slot)
                    for q in range(QT - 1):
                        p_transpose(n, k, q, static_n == 0)
                    if next_slot is not None:
                        scores(pe, n + 1, 1 - k, next_slot, 2, (n + 1) * QT + 2)
                    p_transpose(n, k, QT - 1, static_n == 0)
                    if ahead_slot is not None and (unit is not None or chunk is not None or extra is not None):
                        pe.wait_ge(g_lo_done, n + 3)
                    if z_end is not None:
                        natural_z(z_end)
                        open_z()
                    elif unit is not None:
                        v_unit(*unit)
                    if extra is not None:
                        extra()
                    if chunk is not None:
                        yt_chunk(chunk, ps_g)
                    if before:
                        if v_guard is not None:
                            pe.wait_ge(v3_done, v_guard)
                        if static_n is None:
                            pe.wait_ge(y_done, n - 1)
                        pv(n - 1, h - 1, 1 - k, slot if before_slot is None else before_slot)
                    if z_end is not None:
                        pe.wait_ge(ln1_step, LN_STEPS * z_end + 1)
                        v_unit(*unit)

                def v_unit(b, j):
                    pe.wait_ge(xv_in, (b * UNITS + j + 1) * 16)
                    three_passes(ps_g[:, :], [xv[:, q, :] for q in range(2)],
                                 [vt[:, q, bass.ds(j // QT * BANK, BANK)] for q in range(2)]).then_inc(v_filled, 1)

                def natural_z(b):
                    pe.wait_ge(zt_done, b + 1)
                    for t in range(QT):
                        ins = nc.tensor.transpose(ps_g[:, t * P:(t + 1) * P], col[:, t * P:(t + 1) * P], ident[:, :])
                    ins.then_inc(zn_filled, 1)

                def start():
                    pe.sem_inc(g_filled, 2)
                    pe.sem_inc(v_filled, UNITS)
                    open_z()
                    step(0, 0, 0, 0, next_slot=0, ahead_slot=0, before=False, static_n=0)
                    step(1, 1, 1, 0, next_slot=0, ahead_slot=0, static_n=1)
                    step(2, 0, 2, 0, next_slot=0, ahead_slot=0)
                    step(3, 1, 3, 0, next_slot=0, ahead_slot=0, chunk=0)

                def v_split(b, j):
                    return b * UNITS + j + V_BASE + 1

                def pair(b, i, last, final):
                    n = b * H + 2 * i
                    slot, other = b % 2, (b + 1) % 2
                    if last and not final:
                        pe.wait_ge(xt_in, (b + 1) * 16)
                    ahead = (None if final else other) if last else slot
                    pe.wait_ge(v3_done, b * UNITS + V_BASE)
                    step(n, 0, 2 * i, slot, next_slot=slot, ahead_slot=ahead, unit=None if final else (b, i - 2),
                         z_before=b * HP + i - 2, extra=first_extra(i, last) if final else None)
                    if final and isinstance(i, int):
                        pe.wait_ge(gate_step if last else x1t_done, 1)
                    step(n + 1, 1, 2 * i + 1, slot, next_slot=ahead, ahead_slot=ahead,
                         free_g=None if final else v_split(b, i - 2), chunk=b * HP + i - 1)

                def first_pair(b):
                    n = (b + 1) * H
                    slot, other = b % 2, (b + 1) % 2
                    step(n, 0, H, other, next_slot=other, ahead_slot=other, before_slot=slot, unit=(b, UNITS - 2),
                         z_before=(b + 1) * HP - 2)
                    step(n + 1, 1, 1, other, next_slot=other, ahead_slot=other, free_g=v_split(b, UNITS - 2),
                         v_guard=b * UNITS + QT + V_BASE, chunk=(b + 1) * HP - 1)

                def second_pair(b):
                    n = (b + 1) * H + 2
                    other = (b + 1) % 2
                    step(n, 0, 2, other, next_slot=other, ahead_slot=other, unit=(b, UNITS - 1),
                         z_before=(b + 1) * HP - 1, z_end=b)
                    step(n + 1, 1, 3, other, next_slot=other, ahead_slot=other, free_g=v_split(b, UNITS - 1),
                         chunk=(b + 1) * HP)

                def x1_transpose(b):
                    pe.wait_ge(x1_in, 16 * (b + 1))
                    for t in range(QT):
                        ins = nc.tensor.transpose(ps_g[:, t * P:(t + 1) * P], x1_fix[:, t * P:(t + 1) * P],
                                                  ident[:, :])
                    ins.then_inc(x1t_filled, 1)

                def logits(b):
                    pe.wait_ge(x1t_done, b + 1)
                    for t in range(QT):
                        ins = nc.tensor.matmul(logit_bank(b)[:, t * E:(t + 1) * E], x1t[:, t * P:(t + 1) * P],
                                               wg[:, :], start=True, stop=True)
                    ins.then_inc(logit_filled, 1)

                def comb_transpose(b):
                    pe.wait_ge(gate_step, GATE_STEPS * (b + 1))
                    for t in range(QT):
                        ins = nc.tensor.transpose(rows_bank(b)[0:2 * E, t * P:(t + 1) * P],
                                                  comb_parts[:, t, :].bitcast(F32), ident[:, :])
                    ins.then_inc(ct_filled, 1)

                def first_extra(i, last):
                    if not isinstance(i, int):
                        return None
                    return first_logits if last else (lambda: x1_transpose(0))

                def first_logits():
                    pe.wait_ge(in_wg, 16)
                    logits(0)

                def up(b, s):
                    if s % FT == 0:
                        pe.wait_ge(x1t_lo_done, b + s // FT + 1)
                    if not isinstance(b, int) or b > 0 or s >= RING:
                        pe.wait_ge(hid_done, FT * b + s - RING + 1)
                    f = s % FT
                    three_passes(up_bank[s % RING], [w1[:, c, f * P:(f + 1) * P] for c in range(2)],
                                 [x1t_parts[:, (b + s // FT) % 2, c, :] for c in range(2)]).then_inc(up_filled, 1)

                def end():
                    n = B * H - 1
                    pe.wait_ge(w_lo, 2 * 2)
                    pe.wait_ge(pt_lo_done, 2 * n + 1)
                    up(0, 0)
                    pe.wait_ge(y_done, n)
                    pv(n, H - 1, 1, (B - 1) % 2)
                    z_product(B * HP - 2, False)
                    pe.wait_ge(max_done, B * H * QT)
                    comb_transpose(0)
                    yt_chunk(B * HP - 1, ps_g)
                    up(0, 1)
                    up(0, 2)

                attention(pe, start, pair, first_pair, second_pair, end)

                def weights_row(b, e):
                    if e % E == 0:
                        pe.wait_ge(ct_done, b + e // E + 1)
                    if not isinstance(b, int) or b > 0 or e >= 1:
                        pe.wait_ge(c_done, E * b + e)
                    nc.tensor.matmul(row_bank, sel[:, e % E * P:(e % E + 1) * P], ct[:, :], start=True,
                                     stop=True).then_inc(c_filled, 1)

                def down(b, s):
                    pe.wait_ge(hid_lo_done, FT * b + s + 1)
                    if s == 0:
                        pe.wait_ge(zt_done, B)
                    if s == FT:
                        pe.wait_ge(col2_done, b + 1)
                    f = s % FT
                    three_passes(ps_z[:, :], [w2[:, c, f * P:(f + 1) * P] for c in range(2)],
                                 [hid_hi[s % RING], hid_lo[s % RING]], start=f == 0,
                                 stop=f == FT - 1).then_inc(down_step, 1)

                def stage(b, s, final):
                    if s < FT or not final:
                        if s >= LAG:
                            up(b, s)
                        if s == 0:
                            weights_row(b, 0)
                            z_product(B * HP - 1, True)
                        if s % FPE == 1 and (s + 1 < FT or not final):
                            weights_row(b, (s + 1) // FPE)
                        if s == 1:
                            natural_z(B - 1)
                            pe.wait_ge(w_lo, 2 * E)
                    if s >= LAG:
                        down(b, s - LAG)
                    if not final and s == PREP_X1T:
                        pe.wait_ge(zn_taken, B + 1)
                        pe.wait_ge(on_taken, b + 1)
                        x1_transpose(b + 1)
                    if not final and s == PREP_X1T + 2:
                        logits(b + 1)
                    if not final and s == PREP_ROWS:
                        comb_transpose(b + 1)
                    if s == FT + OUT_AT - final:
                        pe.wait_ge(col2_done, b + 1)
                        for t in range(QT):
                            ins = nc.tensor.transpose(ps_g[:, t * P:(t + 1) * P], col[:, t * P:(t + 1) * P],
                                                      ident[:, :])
                        ins.then_inc(on_filled, 1)

                pe.wait_ge(sel_step, 4)
                experts(pe, stage)


_INS = ['L0_attn_x', 'L0_attn_Q', 'L0_attn_K', 'L0_attn_V', 'L0_attn_W', 'L0_ffn_Wg', 'L0_ffn_W1', 'L0_ffn_W2']
_OUTS = [((4, 512, 128), 'float32')]


def kernel(**inputs):
    import numpy as _np
    import concourse.bacc as _bacc
    from concourse import mybir as _mybir
    from concourse.bass_utils import run_bass_kernel_spmd as _run

    nc = _bacc.Bacc("TRN2", target_bir_lowering=False, num_devices=1)
    arrays, args = {}, []
    for name in _INS:
        a = _np.ascontiguousarray(inputs[name])
        arrays[f"in_{name}_dram"] = a
        args.append(nc.dram_tensor(f"in_{name}_dram", a.shape, _mybir.dt.from_np(a.dtype), kind="ExternalInput").ap())
    for i, (shape, dtype) in enumerate(_OUTS):
        dt = _mybir.dt.from_np(_np.dtype(dtype))
        args.append(nc.dram_tensor(f"out_{i}_dram", shape, dt, kind="ExternalOutput").ap())
    post_ln_layer(nc, *args)
    r = _run(nc, [arrays], core_ids=[0])
    got = tuple(r.results[0][f"out_{i}_dram"] for i in range(len(_OUTS)))
    return got[0]
```
